# Optimizing a Trainium2 kernel written in Bass

```python
import numpy as np
import jax
import jax.numpy as jnp

def _softmax(x, axis=-1):
    return jax.nn.softmax(x, axis=axis)

def _gelu(x):
    return jax.nn.gelu(x, approximate=True)

def _silu(x):
    return jax.nn.silu(x)

def _sigmoid(x):
    return jax.nn.sigmoid(x)

def _layernorm(x, axis=-1, eps=1e-05):
    m = jnp.mean(x, axis=axis, keepdims=True)
    v = jnp.var(x, axis=axis, keepdims=True)
    return (x - m) / jnp.sqrt(v + eps)

def _scatter_add(tgt, idx, src, axis=0):
    return tgt.at[idx].add(src)

def _segment_sum(src, seg, n):
    return jax.ops.segment_sum(src, seg, n)
kernel_name = 'mk_vit_tower_d1_tok_img768_r4_1faef9'

def setup_inputs(seed: int=0):
    np.random.seed(seed)
    _w = jnp.asarray

    def _rec_inputs():
        import jax
        import jax.numpy as jnp
        _rk = jax.random.key(seed)
        x = -0.000147625 + 0.999875 * jax.random.normal(jax.random.fold_in(_rk, 1), (64, 12, 224, 224), jnp.float32)
        return x
    x = _rec_inputs()

    def _L0_tok_setup():
        import jax, jax.numpy as jnp
        import numpy as np
        IMG = 224
        PATCH = 16
        EMBED = 192
        C = 12
        B = 64
        key = jax.random.key(seed)
        k1, k2 = jax.random.split(key)
        x = jax.random.normal(k1, (B, C, IMG, IMG), dtype=jnp.float32)
        channel_weights = jax.random.normal(k2, (C, EMBED), dtype=jnp.float32)
        return {'x': x, 'channel_weights': channel_weights}
    _L0_tok_all = _L0_tok_setup()
    _L0_tok_in = {k: v for k, v in _L0_tok_all.items() if k in ('channel_weights',)}
    del _L0_tok_all

    def _L0_attn_setup():
        import jax, jax.numpy as jnp
        import numpy as np
        key = jax.random.key(seed)
        ks = jax.random.split(key, 4)
        B, S, D = (8, 512, 192)
        lim = (6.0 / (D + D)) ** 0.5
        Z = jax.random.normal(ks[0], (B, S, D), dtype=jnp.float32)
        Wq = jax.random.uniform(ks[1], (D, D), dtype=jnp.float32, minval=-lim, maxval=lim)
        Wk = jax.random.uniform(ks[2], (D, D), dtype=jnp.float32, minval=-lim, maxval=lim)
        Wv = jax.random.uniform(ks[3], (D, D), dtype=jnp.float32, minval=-lim, maxval=lim)
        bq = jnp.zeros((D,), dtype=jnp.float32)
        bk = jnp.zeros((D,), dtype=jnp.float32)
        bv = jnp.zeros((D,), dtype=jnp.float32)
        return {'Z': Z, 'Wq': Wq, 'bq': bq, 'Wk': Wk, 'bk': bk, 'Wv': Wv, 'bv': bv}
    _L0_attn_all = _L0_attn_setup()
    _L0_attn_in = {k: v for k, v in _L0_attn_all.items() if k in ('Wq', 'bq', 'Wk', 'bk', 'Wv', 'bv')}
    del _L0_attn_all

    def _L0_ffn_setup():
        import jax, jax.numpy as jnp
        import numpy as np
        DIM = 192
        NUM_EXPERTS = 4
        NUM_HEADS = 12
        HEAD_DIM = DIM // NUM_HEADS
        MLP_HID = 4 * DIM
        FC1_OUT = MLP_HID + 3 * DIM
        FC2_IN = MLP_HID + DIM
        FC2_OUT = 2 * DIM
        CAP_FACTOR = 0.5
        LN_EPS = 1e-06
        key = jax.random.key(seed)
        ks = jax.random.split(key, 4)
        B, N = (8, 256)
        return {'x': jax.random.normal(ks[0], (B, N, DIM), jnp.float32), 'w_router': jax.random.normal(ks[1], (NUM_EXPERTS, DIM), jnp.float32) * 0.02, 'gamma1': jnp.ones((DIM,), jnp.float32), 'beta1': jnp.zeros((DIM,), jnp.float32), 'w1': jax.random.normal(ks[2], (FC1_OUT, DIM), jnp.float32) * 0.02, 'b1': jnp.zeros((FC1_OUT,), jnp.float32), 'w2': jax.random.normal(ks[3], (FC2_OUT, FC2_IN), jnp.float32) * 0.02, 'b2': jnp.zeros((FC2_OUT,), jnp.float32)}
    _L0_ffn_all = _L0_ffn_setup()
    _L0_ffn_in = {k: v for k, v in _L0_ffn_all.items() if k in ('w_router', 'gamma1', 'beta1', 'w1', 'b1', 'w2', 'b2')}
    del _L0_ffn_all
    return {'x': x, 'L0_tok_channel_weights': _L0_tok_in['channel_weights'], 'L0_attn_Wq': _L0_attn_in['Wq'], 'L0_attn_bq': _L0_attn_in['bq'], 'L0_attn_Wk': _L0_attn_in['Wk'], 'L0_attn_bk': _L0_attn_in['bk'], 'L0_attn_Wv': _L0_attn_in['Wv'], 'L0_attn_bv': _L0_attn_in['bv'], 'L0_ffn_w_router': _L0_ffn_in['w_router'], 'L0_ffn_gamma1': _L0_ffn_in['gamma1'], 'L0_ffn_beta1': _L0_ffn_in['beta1'], 'L0_ffn_w1': _L0_ffn_in['w1'], 'L0_ffn_b1': _L0_ffn_in['b1'], 'L0_ffn_w2': _L0_ffn_in['w2'], 'L0_ffn_b2': _L0_ffn_in['b2']}

def reference(x, L0_tok_channel_weights, L0_attn_Wq, L0_attn_bq, L0_attn_Wk, L0_attn_bk, L0_attn_Wv, L0_attn_bv, L0_ffn_w_router, L0_ffn_gamma1, L0_ffn_beta1, L0_ffn_w1, L0_ffn_b1, L0_ffn_w2, L0_ffn_b2):
    import jax
    import jax.numpy as jnp

    def _L0_tok_ref(x, channel_weights):
        import jax, jax.numpy as jnp
        import numpy as np
        IMG = 224
        PATCH = 16
        EMBED = 192
        C = 12
        B = 64
        Bb, Cc, H, W = x.shape
        K = PATCH
        n = H // K
        pooled = x.reshape(Bb, Cc, n, K, n, K).sum(axis=(3, 5))
        out = jnp.einsum('bcij,ce->bije', pooled, channel_weights)
        return out.reshape(Bb, n * n, EMBED)

    def _L0_attn_ref(Z, Wq, bq, Wk, bk, Wv, bv):
        import jax, jax.numpy as jnp
        import numpy as np
        D = Z.shape[-1]
        scale = 1.0 / D ** 0.5
        Q = jnp.einsum('bsd,ed->bse', Z, Wq) + bq
        K = jnp.einsum('bsd,ed->bse', Z, Wk) + bk
        V = jnp.einsum('bsd,ed->bse', Z, Wv) + bv
        scores = jnp.einsum('bqd,bkd->bqk', Q, K) * scale
        attn = jax.nn.softmax(scores, axis=-1)
        Z_hat = jnp.einsum('bqk,bkd->bqd', attn, V)
        return Z_hat

    def _L0_ffn_ref(x, w_router, gamma1, beta1, w1, b1, w2, b2):
        import jax, jax.numpy as jnp
        import numpy as np
        DIM = 192
        NUM_EXPERTS = 4
        NUM_HEADS = 12
        HEAD_DIM = DIM // NUM_HEADS
        MLP_HID = 4 * DIM
        FC1_OUT = MLP_HID + 3 * DIM
        FC2_IN = MLP_HID + DIM
        FC2_OUT = 2 * DIM
        CAP_FACTOR = 0.5
        LN_EPS = 1e-06
        B, N, C = x.shape
        E = NUM_EXPERTS
        cap = int(CAP_FACTOR * N)
        m = np.array([C // 2 ** (E - 1 - e) for e in range(E)])
        in_mask = (np.arange(C)[None, :] < m[:, None]).astype(np.float32)
        in_mask = jnp.asarray(in_mask)
        out_mask = jnp.concatenate([in_mask, in_mask], axis=-1)
        logits = jnp.einsum('bnc,ec->bne', x, w_router)
        probs = jax.nn.softmax(logits, axis=-1)
        gate, idx = jax.lax.top_k(jnp.swapaxes(probs, 1, 2), cap)
        dispatch = jax.nn.one_hot(idx, N, dtype=x.dtype)
        combine = dispatch * gate[..., None]
        mu = jnp.mean(x, -1, keepdims=True)
        var = jnp.var(x, -1, keepdims=True)
        y = (x - mu) * jax.lax.rsqrt(var + LN_EPS) * gamma1 + beta1
        xg = jnp.einsum('becn,bnd->becd', dispatch, y)
        xg = xg * in_mask[None, :, None, :]
        h = jnp.einsum('becd,fd->becf', xg, w1) + b1
        h = jnp.einsum('becn,becf->bnf', dispatch, h)
        x_mlp, x_qkv = (h[..., :MLP_HID], h[..., MLP_HID:])
        qkv = x_qkv.reshape(B, N, 3, NUM_HEADS, HEAD_DIM).transpose(2, 0, 3, 1, 4)
        q, k, v = (qkv[0], qkv[1], qkv[2])
        scale = HEAD_DIM ** (-0.5)
        attn = jax.nn.softmax(jnp.einsum('bhqd,bhkd->bhqk', q, k) * scale, axis=-1)
        x_attn = jnp.einsum('bhqk,bhkd->bhqd', attn, v)
        x_attn = x_attn.transpose(0, 2, 1, 3).reshape(B, N, C)
        x_mlp = jax.nn.gelu(x_mlp, approximate=False)
        y2 = jnp.concatenate([x_mlp, x_attn], axis=-1)
        yg = jnp.einsum('becn,bnf->becf', dispatch, y2)
        o = jnp.einsum('becf,of->beco', yg, w2) + b2
        o = o * out_mask[None, :, None, :]
        z = jnp.einsum('becn,beco->bno', combine, o)
        x_mlp2, x_attn2 = (z[..., :C], z[..., C:])
        return x + x_mlp2 + x_attn2
    h = _L0_tok_ref(x, L0_tok_channel_weights)
    h = h + _L0_attn_ref(_layernorm(h, axis=-1), L0_attn_Wq, L0_attn_bq, L0_attn_Wk, L0_attn_bk, L0_attn_Wv, L0_attn_bv)
    h = h + _L0_ffn_ref(_layernorm(h, axis=-1), L0_ffn_w_router, L0_ffn_gamma1, L0_ffn_beta1, L0_ffn_w1, L0_ffn_b1, L0_ffn_w2, L0_ffn_b2)
    return h

_drawn_inputs = setup_inputs


def setup_inputs(seed=0):
    import zlib

    import numpy as np

    out = dict(_drawn_inputs(seed))
    spreads = {'L0_attn_bq': (0.0, 0.8),
     'L0_attn_bk': (0.0, 2.0),
     'L0_attn_bv': (0.0, 2.0),
     'L0_ffn_gamma1': (1.0, 0.6),
     'L0_ffn_beta1': (0.0, 0.8),
     'L0_ffn_b1': (0.0, 0.8),
     'L0_ffn_b2': (0.0, 2.0)}
    factors = {'L0_attn_Wq': 8.0,
     'L0_attn_Wk': 8.0,
     'L0_attn_Wv': 8.0,
     'L0_ffn_w_router': 8.0,
     'L0_ffn_w1': 8.0,
     'L0_ffn_w2': 8.0}
    for name, (base, spread) in spreads.items():
        noise = np.random.default_rng([zlib.crc32(name.encode()), seed]).standard_normal(out[name].shape)
        drawn = base * np.exp(spread * noise) if base else spread * noise
        out[name] = jnp.asarray(drawn.astype(out[name].dtype))
    for name, factor in factors.items():
        out[name] = (out[name] * factor).astype(out[name].dtype)
    return out
```

```python
from contextlib import ExitStack

import numpy as np

import concourse.bass as bass
from concourse import mybir

ALU = mybir.AluOpType
ACT = mybir.ActivationFunctionType
AX = mybir.AxisListType
F32 = mybir.dt.float32
F16 = mybir.dt.float16

C, SIDE, PATCH = 12, 224, 16
GRID = SIDE // PATCH
T = GRID * GRID
HT = T // 2
D = 192
DC = D // 2
E = 4
CAP = T // 2
H, DH = 12, 16
HID = 4 * D
F1 = HID + 3 * D
NF = HID // 128
Z = 2 * C + 1
ZS = Z + 1
U = E * ZS
GRP = 8
QUAD = 4
PAIR = 2
TILES = 3
PLANES = PAIR * C // TILES
PP = PLANES * GRID
XROW = PATCH * SIDE
NX = 3
NSTACK = 4
KS = 96
MISC = 4
ONE = 1
W_LOADS = 20
NP = 4
REPLACED = -1.0

CONST = {}
_at = 0
for _name, _w in (("ident", 128), ("plane", TILES * PAIR * C), ("den", 128), ("mask8", 128), ("one13", 128),
                  ("mask4", 4 * 32 + 4 * 5), ("col8", GRP), ("col4", QUAD), ("rep25", 128), ("rep13", 128),
                  ("rep12", 24), ("mask2", 24), ("emask", 2 * E), ("last", U), ("rowsel", GRID), ("half", 16)):
    CONST[_name] = (_at, _w)
    _at += _w
NCONST = _at


def constants():
    c = np.zeros((128, NCONST), np.float32)

    def put(name, a):
        a = np.asarray(a, np.float32)
        at, w = CONST[name]
        c[: a.shape[0], at:at + w] = a.reshape(a.shape[0], w)

    p, q = np.arange(128)[:, None], np.arange(128)[None, :]
    put("ident", p == q)
    plane = np.zeros((PP, TILES, PAIR * C))
    for t in range(TILES):
        for r in range(PP):
            plane[r, t, t * PLANES + r // GRID] = 1
    put("plane", plane)
    put("den", (p // 32 == q // 32) & (p % 32 == DH))
    put("mask8", p // 16 == q // 16)
    put("one13", (p == q) & (p % 16 == 13))
    j = np.arange(148)[None, :]
    put("mask4", np.where(j < 128, p // 32 == j // 32, p // 32 == (j - 128) // 5))
    put("col8", p // 16 == np.arange(GRP)[None, :])
    put("col4", p // 32 == np.arange(QUAD)[None, :])
    put("rep25", (q % 32 == p)[:Z])
    put("rep13", (q % 16 == p)[:13])
    k = np.arange(24)
    put("rep12", (k[None, :] % 12 == np.arange(12)[:, None]))
    put("mask2", k[None, :] // 12 == k[:, None] // 12)
    d = np.arange(DC)[:, None, None] + DC * np.arange(2)[None, :, None]
    put("emask", d < (D >> (E - 1 - np.arange(E)))[None, None, :])
    put("last", (np.arange(U) % ZS == Z)[None, :])
    put("rowsel", p[:PP] % GRID == np.arange(GRID)[None, :])
    put("half", np.full((128, 16), -0.5))
    return c



def front_steps():
    pool = [[("pool", m), ("tokens", m)] for m in range(GRP // PAIR)]
    first = [("norm1",)] + [("first_max", i) for i in range(GRP)] + [("shift1",)]
    second = []
    for i in range(GRP):
        second.append(("first_exp", i))
        if i:
            second.append(("first_mix", i - 1))
        if i == QUAD:
            second.append(("stream", 0))
    second.append(("first_mix", GRP - 1))
    stream = [("stream", 1), ("gates",)]
    chosen = [("choose", k) for k in range(3)] + [("chosen",)]
    return pool + [first, second, stream, chosen]


def body(with_next):
    ops = []
    steps = front_steps() if with_next else [[] for _ in range(8)]
    if with_next:
        ops.append(("load", 1))
    ops.append(("spread", 0))
    for i in range(GRP):
        ops.append(("turn_u", 0, i))
    for i in range(GRP):
        ops.append(("hidden", 0, i))
        if i == 0:
            ops.append(("project", 0, 0))
        if i == 2:
            ops.append(("project", 0, 1))
        if i == 4:
            ops.append(("values", 0, 0))
            ops += [("peak", 0, 0, h) for h in range(6)]
        if i == 5:
            ops.append(("shift", 0, 0, 0))
            ops += [("peak", 0, 0, h) for h in range(6, H)]
        if i == 6:
            ops.append(("shift", 0, 0, 1))
        ops.append(("residual", 0, i))
    for i in range(GRP):
        fill = [[] for _ in range(H)]
        nxt = [(op[0], 1) + op[1:] for op in steps[i]]
        for n, op in enumerate(nxt):
            fill[n * H // max(len(nxt), 1)].append(op)
        if i:
            fill[1] += [("norm", 0, i - 1, 2)]
            fill[0] += [("shift", 0, i, 1)]
            for k in range(4):
                fill[2 + k].append(("fc2", 0, i - 1, k))
        fill[6].append(("norm", 0, i, 0))
        fill[9].append(("norm", 0, i, 1))
        if i + 1 < GRP:
            fill[6].append(("shift", 0, i + 1, 0))
            fill[8].append(("values", 0, i + 1))
        if i + 2 < GRP:
            fill[7].append(("project", 0, i + 2))
        for h in range(H):
            if i + 1 < GRP:
                ops.append(("peak", 0, i + 1, h))
            ops.append(("score", 0, i, h))
            ops += fill[h]
            if h:
                ops.append(("mix", 0, i, h - 1))
        ops.append(("mix", 0, i, H - 1))
    ops.append(("norm", 0, GRP - 1, 2))
    for k in range(4):
        ops.append(("fc2", 0, GRP - 1, k))
    return ops


def ring_of(op):
    name, key = op[0], op[1:]
    if name == "tokens":
        return [("planes", key), ("tok", key)], [("planes", key), ("tok", key)]
    if name == "norm1":
        return [("aT", key), ("t1", key)], [("aT", key), ("t1", key)]
    if name in ("first_max", "first_exp", "norm", "residual", "turn_u", "values", "gates", "chosen"):
        ks = [(name, key)]
        if name == "norm":
            ks = [("den", key)]
        return ks, ks
    if name == "shift":
        return [("shift", key)], [("shift", key)]
    if name == "shift1":
        return [("xT", key), ("t2", key)], [("xT", key), ("t2", key)]
    if name == "first_mix":
        g, i = key
        k = [("uT", (g, i // QUAD))]
        return (k if i % QUAD == 0 else []), (k if i % QUAD == QUAD - 1 else [])
    if name == "stream":
        ks = [("utok", key), ("zT", key), ("w2", key)]
        return ks, ks
    if name == "hidden":
        ks = [("hid", key + (b,)) for b in range(NF // 2)]
        return ks, ks
    if name == "project":
        ks = [("q", key), ("k", key)]
        return ks, ks
    if name == "mix":
        g, i, h = key
        k = [("O", (g, i, h // 4))]
        return (k if h % 4 == 0 else []), (k if h % 4 == 3 else [])
    if name == "fc2":
        g, i, k = key
        ks = [("B", (g, i))]
        return (ks if k == 0 else []), (ks if k == 3 else [])
    return [], []


def plan_ring(ops):
    place, count, closed_at, open_ = {}, [0] * MISC, [-MISC + s for s in range(MISC)], set()
    for n, op in enumerate(ops):
        opens, closes = ring_of(op)
        for key in opens:
            free = [s for s in range(MISC) if s not in open_]
            slot = min(free, key=lambda s: closed_at[s])
            place[key] = (slot, count[slot])
            count[slot] += 1
            open_.add(slot)
            if key in closes:
                open_.discard(slot)
                closed_at[slot] = 10 * n + 10 + opens.index(key)
        for key in closes:
            if key not in opens:
                open_.discard(place[key][0])
                closed_at[place[key][0]] = 10 * n + 10
    return place, count


LINKS = {"norm1": 3, "shift1": 2, "stream": 3, "gates": 11, "choose": 10, "chosen": 0, "spread": 6, "residual": 0}
CHOOSE = (5, 5, 3)


def link_count(op):
    if op[0] == "choose":
        n = 2 * CHOOSE[op[2]]
        return n + 2 if op[2] == 2 else n
    return LINKS.get(op[0], 0)


def bass_vit_tower(nc, x, cw, Wq, bq, Wk, bk, Wv, bv, w_router, gamma, beta, w1, b1, w2, b2, consts, out):
    B = x.shape[0]
    NG = B // GRP

    sections = {"pro": [], "loop": body(True), "last": body(False)}
    sections["pro"] = [("load", 0)] + [(op[0], 0) + op[1:] for step in front_steps() for op in step]
    rings = {s: plan_ring(ops) for s, ops in sections.items()}
    links = {s: sum(link_count(op) for op in ops) for s, ops in sections.items()}

    ctx = ExitStack()
    with ctx:
        def sb(name, shape, dt=F32):
            return ctx.enter_context(nc.sbuf_tensor(name, shape, dt))

        def sem(name):
            return ctx.enter_context(nc.semaphore(name))

        cst = sb("cst", [128, NCONST])

        def const(name, rows=128):
            at, w = CONST[name]
            return cst[0:rows, at:at + w]

        ident = const("ident")

        xt = sb("xt", [PP, NX, XROW])
        psums = sb("psums", [PP, 2, TILES, GRID])
        spread_p = sb("spread_p", [PP, TILES, GRID, GRID])
        planesT = sb("planesT", [PAIR * C, T])
        wtok = sb("wtok", [HT, 2, GRP, C])
        tmp = sb("tmp", [HT, 2, GRP, 26])
        var = sb("var", [HT, 8, 2 * GRP])
        a_tok = sb("a_tok", [HT, 2, GRP, 32])
        x_tok = sb("x_tok", [HT, 2, GRP, 16])
        aT = sb("aT", [128, T])
        tT = sb("tT", [128, T])
        tm = sb("tm", [128, 2, T])
        nm1 = sb("nm1", [HT, 2, GRP])
        P1 = sb("P1", [HT, 2, 2, T])
        uT = sb("uT", [128, T])
        xT = uT
        urec = sb("urec", [HT, 2, QUAD])
        z_tok = sb("z_tok", [HT, 2, GRP, 32])
        zT = sb("zT", [128, GRP // QUAD, T])
        lg = sb("lg", [HT, 2, GRP, 5])
        soft = sb("soft", [HT, 3, 2 * GRP * E])
        red = sb("red", [HT, 3, 2 * GRP])
        prob = sb("prob", [HT, 2, GRP * E])
        rows = sb("rows", [GRP * E, T])
        top8 = sb("top8", [GRP * E, 8])
        sel = sb("sel", [HT, 2, GRP * E])
        cg = sb("cg", [HT, 2 * GRP, E])
        gate8 = sb("gate8", [HT, 2 * GRP, 8])
        zs = sb("zs", [HT, 2 * GRP, ZS])
        UT = sb("UT", [U, GRP, T])
        hid = sb("hid", [128, GRP, NF, T])
        resid = sb("resid", [HT, GRP, 2, D])
        qk16 = sb("qk16", [DC, 2, 2, 2, T], F16)
        qs = sb("qs", [KS + 1, NSTACK, H, T], F16)
        ks = sb("ks", [KS + 1, NSTACK, H, T], F16)
        vals = sb("vals", [HT, 2, 2, H, 32])
        peaks = sb("peaks", [HT, 2, 2, 6])
        shiftT = sb("shiftT", [6, 2, T], F16)
        late = sb("late", [HT, max(NP * 2 * T, 2 * GRP * U)])
        Pb = late[:, 0:NP * 2 * T].rearrange("p (n q t) -> p n q t", n=NP, q=2)
        u_tok = late[:, 0:2 * GRP * U].rearrange("p (n e z) -> p n e z", n=2 * GRP, e=E)
        oT = sb("oT", [128, 3, T])
        rden = sb("rden", [128, 3, T])
        onT = sb("onT", [128, 3, T])
        fin = sb("fin", [HT, 2, 2, D])
        Abd = sb("Abd", [128, 2, 128])
        WR = sb("WR", [128, 148])
        G4 = sb("G4", [128, QUAD, D])
        WI = sb("WI", [2 * C, 48])
        M = sb("M", [U, F1])
        w2T = sb("w2T", [128, NF + 3, D])

        banks = [ctx.enter_context(nc.psum_tensor(f"bank{b}", [128, 512], F32)) for b in range(8)]
        score_ps = banks[0:2]
        peak_ps = banks[2:4]
        misc_ps = banks[4:8]
        qk_dram = nc.dram_tensor("qk_scratch", (2, 2, 2, 2, DC, T), F16, kind="Internal").ap()

        hflat = hid[:, :, :, :].rearrange("p a b c -> p (a b c)")
        n = 0

        def scratch(rows_, *shape):
            nonlocal n
            w = int(np.prod(shape))
            v = hflat[0:rows_, n:n + w]
            n += w
            if len(shape) == 2:
                v = v.rearrange("p (a b) -> p a b", a=shape[0])
            if len(shape) == 3:
                v = v.rearrange("p (a b c) -> p a b c", a=shape[0], b=shape[1])
            return v

        w1_in = scratch(128, 11, D)
        w2_in = scratch(DC, 4, HID + D)
        w1T = scratch(DC, 2, F1)
        G = scratch(Z, D)
        Gc = scratch(Z, D)
        Vp = scratch(C, D)
        w2_pad = resid[0:DC, :, :, :].rearrange("p a b c -> p (a b c)")[:, 0:2 * (HID + H * 32)] \
            .rearrange("p (o f) -> p o f", o=2)
        wa_in = late[0:DC, 0:3 * 2 * D].rearrange("p (m o d) -> p m o d", m=3, o=2)
        wa_T = UT[0:DC, :, :].rearrange("p i t -> p (i t)")[:, 0:3 * 2 * D].rearrange("p (m o d) -> p m o d", m=3, o=2)
        early = tmp[0:C, :, :, :].rearrange("p a b c -> p (a b c)")
        cw_in = early[:, 0:D]
        cwc = early[:, D:2 * D]
        mean = sb("mean", [Z, 2])
        cwcT = sb("cwcT", [DC, 2, C])
        QKp = sb("QKp", [DC, 2, 2, 13])
        wr_in = wtok[0:E, :, :, :].rearrange("p a b c -> p (a b c)")
        RT = sb("RT", [DC, 2, E])
        GcT = sb("GcT", [DC, 2, Z])
        gb = sb("gb", [DC, 2, 2])
        GgT = sb("GgT", [DC, 2, ZS])
        L = P1[0:DC, :, :, :].rearrange("p a b c -> p (a b c)")[:, 0:2 * U].rearrange("p (c e z) -> p c e z", c=2, e=E)
        b1_in = M[0:1, :]
        b2_in = rden[0:1, :, :].rearrange("p a b -> p (a b)")[:, 0:3 * D].rearrange("p (a b) -> p a b", a=3)
        A_rep = sb("A_rep", [13, 8, 16])
        S_rep = soft[0:Z, :, :].rearrange("p a b -> p (a b)")[:, 0:148]
        S12 = sb("S12", [C, 24])

        w_in = sem("w_in")
        gp_in = sem("gp_in")
        cst_in = sem("cst_in")
        zeroed = sem("zeroed")
        zeroed_dve = sem("zeroed_dve")
        turn_full, turn_free = sem("turn_full"), sem("turn_free")
        su_dve, su_pe, su_act, su_dma = sem("su_dve"), sem("su_pe"), sem("su_act"), sem("su_dma")
        bias_in = sem("bias_in")
        misc_full = [sem(f"misc_full{s}") for s in range(MISC)]
        misc_free = [sem(f"misc_free{s}") for s in range(MISC)]
        peak_full = [sem(f"peak_full{s}") for s in range(2)]
        peak_free = [sem(f"peak_free{s}") for s in range(2)]
        score_full = [sem(f"score_full{s}") for s in range(2)]
        score_free = [sem(f"score_free{s}") for s in range(2)]
        probs_used = [sem(f"probs_used{s}") for s in range(NP)]
        x_in = [sem(f"x_in{s}") for s in range(NX)]
        pooled, masked = sem("pooled"), sem("masked")
        planes_out = sem("planes_out")
        tokens_out = sem("tokens_out")
        dve_pow, gp_pow = sem("dve_pow"), sem("gp_pow")
        a_ready, aT_ready, tT_ready = sem("a_ready"), sem("aT_ready"), sem("tT_ready")
        tm_ready = sem("tm_ready")
        max1 = sem("max1")
        x_ready = sem("x_ready")
        P1_ready = sem("P1_ready")
        uT_ready = sem("uT_ready")
        z_ready, zT_ready = sem("z_ready"), sem("zT_ready")
        gates_in, gates_exp = sem("gates_in"), sem("gates_exp")
        prob_ready, sel_rows, sel_ready = sem("prob_ready"), sem("sel_rows"), sem("sel_ready")
        u_ready = sem("u_ready")
        UT_ready = sem("UT_ready")
        hid_ready = sem("hid_ready")
        resid_ready = sem("resid_ready")
        hi_ready, lo_ready = sem("hi_ready"), sem("lo_ready")
        qk_out = sem("qk_out")
        stack_in = [sem(f"stack_in{s}") for s in range(NSTACK)]
        vals_ready = sem("vals_ready")
        peaks_ready = sem("peaks_ready")
        shift_ready = sem("shift_ready")
        shift_in = [sem(f"shift_in{s}") for s in range(2)]
        oT_ready = sem("oT_ready")
        rden_ready, onT_ready = sem("rden_ready"), sem("onT_ready")
        gated, fin_ready = sem("gated"), sem("fin_ready")
        out_done = [sem(f"out_done{s}") for s in range(2)]
        link = sem("link")
        waited = sem("waited")

        block = ctx.enter_context(nc.Block())

        class At:

            def __init__(self, section, g):
                self.section, self.g = section, g
                self.place, self.per = rings[section]
                before = {"pro": [], "loop": ["pro"], "last": ["pro"]}[section]
                self.turns = g if section == "loop" else (NG - 1 if section == "last" else 0)
                self.base = [sum(rings[s][1][k] for s in before) for k in range(MISC)]
                self.loop_per = rings["loop"][1]
                self.link_base = links["pro"] * len(before)
                self.links = 0

            def uses(self, key):
                slot, k = self.place[key]
                return slot, self.turns * self.loop_per[slot] + self.base[slot] + k

            def link_at(self, k):
                return self.turns * links["loop"] + self.link_base + self.links + k

        def run(eng, steps):
            def walk(section, g):
                at = At(section, g)
                for op in sections[section]:
                    if op[0] in steps:
                        steps[op[0]](at, g + op[1], *op[1:])
                    at.links += link_count(op)

            walk("pro", 0)
            if NG > 1:
                with eng.Fori(0, NG - 1) as g:
                    walk("loop", g)
            walk("last", NG - 1)

        def settled(eng):
            eng.sem_inc(waited, 1)

        turns = []
        for m in range(3):
            turns.append(([(wa_in[:, m, o, DC * c:DC * c + DC], DC * (2 * c + o), DC, DC)
                           for c in range(2) for o in range(2)], wa_T[:, m, :, :].rearrange("p c e -> p (c e)")))
        turns.append(([(wr_in[:, DC * c:DC * c + DC], E * c, E, DC) for c in range(2)],
                      RT[:, :, :].rearrange("p c e -> p (c e)")))
        turns.append(([(cwc[:, DC * c:DC * c + DC], C * c, C, DC) for c in range(2)],
                      cwcT[:, :, :].rearrange("p c e -> p (c e)")))
        for c in range(2):
            for f0 in range(0, 11, 4):
                fs = range(f0, min(f0 + 4, 11))
                end = min(128 * (fs[-1] + 1), F1)
                turns.append(([(w1_in[0:min(128, F1 - 128 * f), f, DC * c:DC * c + DC], 128 * (f - f0),
                                min(128, F1 - 128 * f), DC) for f in fs], w1T[:, c, 128 * f0:end]))
        for f0 in range(0, NF + 3, 2):
            fs = range(f0, min(f0 + 2, NF + 3))
            turns.append(([(w2_pad[:, o, 128 * f:128 * f + 128], D * (f - f0) + DC * o, DC, 128)
                           for f in fs for o in range(2)],
                          w2T[:, f0:fs[-1] + 1, :].rearrange("p f o -> p (f o)")))
        turns.append(([(Gc[:, DC * c:DC * c + DC], Z * c, Z, DC) for c in range(2)],
                      GcT[:, :, :].rearrange("p c e -> p (c e)")))
        NT = len(turns)

        @block.sync
        def _(sp):
            for s in [*peak_free, *score_free, *probs_used, *shift_in, *out_done, qk_out, gated, onT_ready, fin_ready]:
                sp.sem_inc(s, ONE)
            sp.dma_start(cst[:, :], consts).then_inc(cst_in, 16)
            for m, w in enumerate((Wq, Wk, Wv)):
                sp.dma_start(wa_in[:, m, :, :], w.rearrange("(o p) d -> p o d", p=DC)).then_inc(w_in, 16)
            sp.dma_start(cw_in[:, :], cw).then_inc(w_in, 16)
            sp.dma_start(G[0:C, :], cw).then_inc(w_in, 16)
            sp.dma_start(G[2 * C:Z, :], bv.rearrange("(a d) -> a d", a=1)).then_inc(w_in, 16)
            for m, b in enumerate((bq, bk)):
                for c in range(2):
                    sp.dma_start(QKp[:, m, c, 12:13], b[DC * c:DC * c + DC].rearrange("(p a) -> p a", a=1)) \
                        .then_inc(w_in, 16)
            sp.dma_start(wr_in[:, :], w_router).then_inc(w_in, 16)
            for m, b in enumerate((gamma, beta)):
                for c in range(2):
                    sp.dma_start(gb[:, m, c:c + 1], b[DC * c:DC * c + DC].rearrange("(p a) -> p a", a=1)) \
                        .then_inc(w_in, 16)
            sp.dma_start(w1_in[:, 0:10, :], w1[0:1280, :].rearrange("(f p) d -> p f d", p=128)).then_inc(w_in, 16)
            sp.dma_start(w1_in[0:F1 - 1280, 10, :], w1[1280:F1, :]).then_inc(w_in, 16)
            sp.dma_start(w2_in[:, :, :], w2.rearrange("(o p) f -> p o f", p=DC)).then_inc(w_in, 16)
            sp.dma_start(b1_in, b1.rearrange("(a f) -> a f", a=1)).then_inc(w_in, 16)
            sp.dma_start(b2_in[:, 0:2, :], b2.rearrange("(a o f) -> a o f", a=1, o=2)).then_inc(w_in, 16)
            sp.wait_ge(su_act, 2)
            sp.dma_start(G[C:2 * C, :], Vp).then_inc(su_dma, 16)
            sp.wait_ge(turn_free, NT - 1)
            sp.wait_ge(su_dve, 4)
            sp.dma_start(w2T[DH:DH + 1, NF, :], b2_in[:, 2, :]).then_inc(bias_in, 16)

            def project(at, G_, dg, i):
                n_ = G_ * GRP + i
                sp.wait_ge(hi_ready, 2 * n_ + 2)
                sp.wait_ge(lo_ready, 2 * n_ + 2)
                sp.dma_start(qk_dram[i % 2].rearrange("m s c p t -> p (m s c) t"),
                             qk16[:, :, :, :, :].rearrange("p m s c t -> p (m s c) t")).then_inc(qk_out, 16)
                sp.wait_ge(qk_out, 16 * n_ + 16 + ONE)
                s = i % NSTACK
                for blk, (qp, kp) in enumerate(((0, 0), (0, 1), (1, 0))):
                    for m, st, part in ((0, qs, qp), (1, ks, kp)):
                        sp.dma_start(st[DH * blk:DH * blk + DH, s, :, :],
                                     qk_dram[i % 2, m, part].rearrange("c (h d) t -> d (c h) t", d=DH)) \
                            .then_inc(stack_in[s], 16)

            def shift(at, G_, dg, i, part):
                n_ = G_ * GRP + i
                sp.wait_ge(shift_ready, 2 * n_ + part + 1)
                sp.dma_start(qs[KS:KS + 1, i % NSTACK, 6 * part:6 * part + 6, :],
                             shiftT[:, part, :]).then_inc(shift_in[part], 16)

            def fc2(at, G_, dg, i, k):
                if k == 3:
                    n_ = G_ * GRP + i
                    sp.wait_ge(fin_ready, n_ + 1 + ONE)
                    sp.dma_start(out[bass.ds(n_, 1)].rearrange("a (h p) d -> p (a h) d", p=HT),
                                 fin[:, i % 2, :, :]).then_inc(out_done[i % 2], 16)

            run(sp, {"project": project, "shift": shift, "fc2": fc2})
            for s in range(2):
                sp.wait_ge(out_done[s], 16 * B // 2 + ONE)

        @block.tensor
        def _(pe):
            pe.wait_ge(cst_in, 16)
            pe.wait_ge(w_in, 16 * W_LOADS)
            for n_, (parts, dst) in enumerate(turns):
                if n_ == 4:
                    pe.wait_ge(su_dve, 1)
                if n_ == 11:
                    pe.wait_ge(su_dve, 2)
                if n_ == NT - 1:
                    pe.wait_ge(turn_free, 5)
                    for m in range(2):
                        for c in range(2):
                            for d in range(2):
                                mm = pe.matmul(banks[0][0:DC, 12 * (2 * m + c):12 * (2 * m + c) + 12],
                                               wa_T[:, m, d, DC * c:DC * c + DC], cwcT[:, d, :],
                                               start=(d == 0), stop=(d == 1))
                    mm.then_inc(su_pe, 1)
                    for d in range(2):
                        mm = pe.matmul(banks[1][0:C, 0:D], cwcT[:, d, :], wa_T[:, 2, d, :],
                                       start=(d == 0), stop=(d == 1))
                    mm.then_inc(su_pe, 1)
                    pe.wait_ge(su_dve, 5)
                if n_ >= MISC:
                    pe.wait_ge(turn_free, n_ - MISC + 1)
                for src, at_, r, w in parts:
                    mm = pe.transpose(misc_ps[n_ % MISC][0:w, at_:at_ + r], src, ident[0:r, 0:r])
                mm.then_inc(turn_full, 1)
            pe.wait_ge(turn_free, NT)
            pe.wait_ge(su_act, 1)
            for c in range(2):
                mm = pe.matmul(banks[2][0:13, 0:13], QKp[:, 0, c, :], QKp[:, 1, c, :],
                               start=(c == 0), stop=(c == 1))
            mm.then_inc(su_pe, 1)
            for c in range(2):
                mm = pe.matmul(banks[3][0:Z, 0:Z], GcT[:, c, :], GcT[:, c, :], start=(c == 0), stop=(c == 1))
            mm.then_inc(su_pe, 1)
            for c in range(2):
                mm = pe.matmul(banks[0][0:Z, 64:64 + E], GcT[:, c, :], RT[:, c, :],
                               start=(c == 0), stop=(c == 1))
            mm.then_inc(su_pe, 1)
            pe.wait_ge(su_dve, 6)
            pe.matmul(banks[1][:, 0:128], const("rep13", 13), A_rep[:, :, :].rearrange("p a b -> p (a b)"),
                      start=True, stop=True).then_inc(su_pe, 1)
            pe.matmul(banks[2][:, 128:276], const("rep25", Z), S_rep[:, :], start=True, stop=True) \
                .then_inc(su_pe, 1)
            pe.matmul(banks[3][:, 128:128 + D], const("rep25", Z), Gc, start=True, stop=True) \
                .then_inc(su_pe, 1)
            pe.matmul(banks[0][0:24, 128:152], const("rep12", C), S12[:, :], start=True, stop=True) \
                .then_inc(su_pe, 1)
            pe.wait_ge(su_dve, 7)
            for n3 in range(3):
                w = F1 // 3
                o = misc_ps[n3][0:U, 0:w]
                for c in range(2):
                    pe.matmul(o, L[:, c, :, :].rearrange("p e z -> p (e z)"), w1T[:, c, w * n3:w * n3 + w],
                              start=(c == 0), stop=False)
                mm = pe.matmul(o, const("last", 1), b1_in[:, w * n3:w * n3 + w], start=False, stop=True)
            mm.then_inc(su_pe, 1)
            pe.wait_ge(su_act, 3)
            pe.wait_ge(su_dve, 8)
            pe.wait_ge(bias_in, 16)
            pe.wait_ge(zeroed, 1)

            def ring(at, *key):
                slot, k = at.uses(key)
                pe.wait_ge(misc_free[slot], k)
                return misc_ps[slot], misc_full[slot]

            def tokens(at, G_, dg, m):
                ps, full = ring(at, "planes", (dg, m))
                pe.wait_ge(masked, 4 * G_ + m + 1)
                for t in range(TILES):
                    mm = pe.matmul(ps[0:PAIR * C, 0:T],
                                   const("plane", PP)[:, PAIR * C * t:PAIR * C * t + PAIR * C],
                                   spread_p[:, t, :, :].rearrange("p a b -> p (a b)"),
                                   start=(t == 0), stop=(t == TILES - 1))
                mm.then_inc(full, 1)
                ps, full = ring(at, "tok", (dg, m))
                pe.wait_ge(planes_out, 4 * G_ + m + 1)
                for h in range(2):
                    mm = pe.matmul(ps[0:HT, 48 * h:48 * h + 48], planesT[:, HT * h:HT * h + HT], WI[:, :],
                                   start=True, stop=True)
                mm.then_inc(full, 1)

            def norm1(at, G_, dg):
                ps, full = ring(at, "aT", (dg,))
                pe.wait_ge(a_ready, G_ + 1)
                for h in range(2):
                    mm = pe.transpose(ps[:, HT * h:HT * h + HT], x_tok[:, h, :, :], ident[0:HT, 0:HT])
                mm.then_inc(full, 1)
                ps, full = ring(at, "t1", (dg,))
                pe.wait_ge(aT_ready, 2 * G_ + 1)
                pe.matmul(ps[:, 0:T], Abd[:, 0, :], aT[:, :], start=True, stop=True).then_inc(full, 1)

            def first_max(at, G_, dg, i):
                ps, full = ring(at, "first_max", (dg, i))
                pe.wait_ge(tm_ready, 2 * GRP * G_ + i + 1)
                for h in range(2):
                    mm = pe.matmul(ps[0:HT, T * h:T * h + T], tm[:, i % 2, HT * h:HT * h + HT], aT[:, :],
                                   start=True, stop=True)
                mm.then_inc(full, 1)

            def shift1(at, G_, dg):
                ps, full = ring(at, "xT", (dg,))
                pe.wait_ge(x_ready, G_ + 1)
                for h in range(2):
                    mm = pe.transpose(ps[:, HT * h:HT * h + HT], x_tok[:, h, :, :], ident[0:HT, 0:HT])
                mm.then_inc(full, 1)
                ps, full = ring(at, "t2", (dg,))
                pe.wait_ge(aT_ready, 2 * G_ + 2)
                pe.matmul(ps[:, 0:T], Abd[:, 1, :], xT[:, :], start=True, stop=True).then_inc(full, 1)

            def first_exp(at, G_, dg, i):
                ps, full = ring(at, "first_exp", (dg, i))
                pe.wait_ge(tm_ready, 2 * GRP * G_ + GRP + i + 1)
                for h in range(2):
                    mm = pe.matmul(ps[0:HT, T * h:T * h + T], aT[:, HT * h:HT * h + HT], tm[:, i % 2, :],
                                   start=True, stop=True)
                mm.then_inc(full, 1)

            def first_mix(at, G_, dg, i):
                j = 32 * (i % QUAD)
                slot, k = at.uses(("uT", (dg, i // QUAD)))
                if i % QUAD == 0:
                    pe.wait_ge(misc_free[slot], k)
                pe.wait_ge(P1_ready, GRP * G_ + i + 1)
                for h in range(2):
                    mm = pe.matmul(misc_ps[slot][j:j + 32, 0:T], a_tok[:, h, i, :], P1[:, i % 2, h, :],
                                   start=(h == 0), stop=(h == 1))
                if i % QUAD == QUAD - 1:
                    mm.then_inc(misc_full[slot], 1)

            def stream(at, G_, dg, q):
                ps, full = ring(at, "utok", (dg, q))
                pe.wait_ge(uT_ready, 2 * G_ + q + 1)
                for h in range(2):
                    mm = pe.transpose(ps[0:HT, 128 * h:128 * h + 128], uT[:, HT * h:HT * h + HT], ident)
                mm.then_inc(full, 1)
                ps, full = ring(at, "zT", (dg, q))
                pe.wait_ge(z_ready, 2 * G_ + q + 1)
                for h in range(2):
                    mm = pe.transpose(ps[:, HT * h:HT * h + HT], z_tok[:, h, QUAD * q:QUAD * q + QUAD, :],
                                      ident[0:HT, 0:HT])
                mm.then_inc(full, 1)
                ps, full = ring(at, "w2", (dg, q))
                pe.wait_ge(zT_ready, 2 * G_ + q + 1)
                for h in range(2):
                    mm = pe.matmul(ps[0:HT, 148 * h:148 * h + 148], zT[:, q, HT * h:HT * h + HT], WR[:, :],
                                   start=True, stop=True)
                mm.then_inc(full, 1)

            def gates(at, G_, dg):
                ps, full = ring(at, "gates", (dg,))
                pe.wait_ge(prob_ready, G_ + 1)
                for h in range(2):
                    mm = pe.transpose(ps[0:GRP * E, HT * h:HT * h + HT], prob[:, h, :], ident[0:HT, 0:HT])
                mm.then_inc(full, 1)

            def chosen(at, G_, dg):
                ps, full = ring(at, "chosen", (dg,))
                pe.wait_ge(sel_rows, G_ + 1)
                settled(pe)
                for h in range(2):
                    mm = pe.transpose(ps[0:HT, 32 * h:32 * h + 32], rows[:, HT * h:HT * h + HT],
                                      ident[0:32, 0:32])
                mm.then_inc(full, 1)

            def turn_u(at, G_, dg, i):
                ps, full = ring(at, "turn_u", (dg, i))
                pe.wait_ge(u_ready, G_ + 1)
                for h in range(2):
                    mm = pe.transpose(ps[0:U, HT * h:HT * h + HT],
                                      u_tok[:, GRP * h + i, :, :], ident[0:HT, 0:HT])
                mm.then_inc(full, 1)

            def residual(at, G_, dg, i):
                ps, full = ring(at, "residual", (dg, i))
                for h in range(2):
                    mm = pe.matmul(ps[0:HT, D * h:D * h + D], zT[:, i // QUAD, HT * h:HT * h + HT],
                                   G4[:, i % QUAD, :], start=True, stop=True)
                mm.then_inc(full, 1)

            def hidden(at, G_, dg, i):
                pe.wait_ge(UT_ready, GRP * G_ + i + 1)
                for b in range(NF // 2):
                    ps, full = ring(at, "hid", (dg, i, b))
                    for j in range(2):
                        f = 2 * b + j
                        mm = pe.matmul(ps[:, T * j:T * j + T], M[:, 128 * f:128 * f + 128], UT[:, i, :],
                                       start=True, stop=True)
                    mm.then_inc(full, 1)

            def project(at, G_, dg, i):
                for n_, m in enumerate("qk"):
                    ps, full = ring(at, m, (dg, i))
                    for c in range(2):
                        f = HID + D * n_ + DC * c
                        mm = pe.matmul(ps[0:DC, T * c:T * c + T], M[:, f:f + DC], UT[:, i, :],
                                       start=True, stop=True)
                    mm.then_inc(full, 1)

            def values(at, G_, dg, i):
                ps, full = ring(at, "values", (dg, i))
                for h in range(2):
                    mm = pe.matmul(ps[0:HT, D * h:D * h + D], UT[:, i, HT * h:HT * h + HT],
                                   M[:, HID + 2 * D:F1], start=True, stop=True)
                mm.then_inc(full, 1)

            def peak(at, G_, dg, i, h):
                s = h % 2
                if h == 0:
                    pe.wait_ge(stack_in[i % NSTACK], 96 * (2 * G_ + i // NSTACK + 1))
                pe.wait_ge(peak_free[s], 6 * (GRP * G_ + i) + h // 2 + ONE)
                for q in range(2):
                    mm = pe.matmul(peak_ps[s][0:HT, T * q:T * q + T],
                                   qs[0:KS, i % NSTACK, h, HT * q:HT * q + HT], ks[0:KS, i % NSTACK, h, :],
                                   start=True, stop=True)
                mm.then_inc(peak_full[s], 1)

            def shift(at, G_, dg, i, part):
                ps, full = ring(at, "shift", (dg, i, part))
                pe.wait_ge(peaks_ready, 2 * (GRP * G_ + i) + part + 1)
                for q in range(2):
                    mm = pe.transpose(ps[0:6, HT * q:HT * q + HT], peaks[:, part, q, :], ident[0:HT, 0:HT])
                mm.then_inc(full, 1)

            def score(at, G_, dg, i, h):
                s = h % 2
                if h % 6 == 0:
                    pe.wait_ge(shift_in[h // 6], 16 * (GRP * G_ + i + 1) + ONE)
                pe.wait_ge(score_free[s], 6 * (GRP * G_ + i) + h // 2 + ONE)
                for k in range(2):
                    mm = pe.matmul(score_ps[s][0:HT, T * k:T * k + T],
                                   ks[:, i % NSTACK, h, HT * k:HT * k + HT], qs[:, i % NSTACK, h, :],
                                   start=True, stop=True)
                mm.then_inc(score_full[s], 1)

            def mix(at, G_, dg, i, h):
                slot, k = at.uses(("O", (dg, i, h // 4)))
                if h % 4 == 0:
                    pe.wait_ge(misc_free[slot], k)
                if h == 0:
                    pe.wait_ge(vals_ready, GRP * G_ + i + 1)
                pe.wait_ge(score_free[h % 2], 6 * (GRP * G_ + i) + h // 2 + 1 + ONE)
                j = 32 * (h % 4)
                for q in range(2):
                    mm = pe.matmul(misc_ps[slot][j:j + 32, 0:T], vals[:, i % 2, q, h, :], Pb[:, h % NP, q, :],
                                   start=(q == 0), stop=(q == 1))
                mm.then_inc(probs_used[h % NP], 1)
                if h % 4 == 3:
                    pe.wait_ge(probs_used[h % NP], 3 * (GRP * G_ + i) + h // NP + 1 + ONE)
                    pe.sem_inc(misc_full[slot], 1)

            def norm(at, G_, dg, i, c):
                ps, full = ring(at, "den", (dg, i, c))
                pe.wait_ge(oT_ready, 3 * (GRP * G_ + i) + c + 1)
                pe.matmul(ps[:, 0:T], const("den"), oT[:, c, :], start=True, stop=True).then_inc(full, 1)

            def fc2(at, G_, dg, i, k):
                slot, n_ = at.uses(("B", (dg, i)))
                if k == 0:
                    pe.wait_ge(misc_free[slot], n_)
                h, parts = k // 2, (range(0, NF) if k % 2 == 0 else range(NF, NF + 3))
                if k == 1:
                    pe.wait_ge(onT_ready, 3 * (GRP * G_ + i) + 3 + ONE)
                for f in parts:
                    lhs = hid[:, i, f, HT * h:HT * h + HT] if f < NF else onT[:, f - NF, HT * h:HT * h + HT]
                    mm = pe.matmul(misc_ps[slot][0:HT, D * h:D * h + D], lhs, w2T[:, f, :],
                                   start=(f == 0), stop=(f == NF + 2))
                if k == 3:
                    mm.then_inc(misc_full[slot], 1)

            run(pe, {"tokens": tokens, "norm1": norm1, "first_max": first_max, "shift1": shift1,
                     "first_exp": first_exp, "first_mix": first_mix, "stream": stream, "gates": gates,
                     "chosen": chosen, "turn_u": turn_u, "residual": residual, "hidden": hidden,
                     "project": project, "values": values, "peak": peak, "shift": shift, "score": score,
                     "mix": mix, "norm": norm, "fc2": fc2})

        @block.scalar
        def _(act):
            for n_, (parts, dst) in enumerate(turns):
                if n_ == NT - 1:
                    act.wait_ge(su_pe, 1)
                    act.copy(QKp[:, :, :, 0:12], banks[0][0:DC, 0:48].rearrange("p (m c k) -> p m c k", m=2, c=2)) \
                        .then_inc(su_act, 1)
                    act.wait_ge(su_pe, 2)
                    act.copy(Vp, banks[1][0:C, 0:D]).then_inc(su_act, 1)
                act.wait_ge(turn_full, n_ + 1)
                rows_ = parts[0][3]
                cols = parts[-1][1] + parts[-1][2]
                act.copy(dst, misc_ps[n_ % MISC][0:rows_, 0:cols]).then_inc(turn_free, 1)
            act.wait_ge(su_pe, 10)
            for n3 in range(3):
                w = F1 // 3
                last = act.copy(M[:, w * n3:w * n3 + w], misc_ps[n3][0:U, 0:w])
            last.then_inc(su_act, 1)

            def ring(at, *key):
                slot, k = at.uses(key)
                act.wait_ge(misc_full[slot], k + 1)
                return misc_ps[slot], misc_free[slot]

            def load_tile(G_, t):
                first_plane = (G_ * (GRP // PAIR) + t // TILES) * PAIR * C + (t % TILES) * PLANES
                act.dma_start(xt[:, t % NX, :],
                              x.rearrange("b c (i k) w -> (b c i) (k w)", k=PATCH)
                              [bass.ds(first_plane * GRID, PP), :]).then_inc(x_in[t % NX], 16)

            def load(at, G_, dg):
                act.wait_ge(pooled, 12 * G_)
                for t in range(NX):
                    load_tile(G_, t)

            def tokens(at, G_, dg, m):
                for t in range(TILES * m, TILES * m + TILES):
                    if t + NX < 12:
                        act.wait_ge(pooled, 12 * G_ + t + 1)
                        load_tile(G_, t + NX)
                ps, free = ring(at, "planes", (dg, m))
                act.copy(planesT[:, :], ps[0:PAIR * C, 0:T]).then_inc(planes_out, 1)
                act.wait_ge(planes_out, 4 * G_ + m + 1)
                act.sem_inc(free, 1)

            def evac(dst, src, free, ready, n_):
                act.copy(dst, src).then_inc(ready, 1)
                act.wait_ge(ready, n_)
                act.sem_inc(free, 1)

            def norm1(at, G_, dg):
                ps, free = ring(at, "aT", (dg,))
                evac(aT[:, :], ps[:, 0:T], free, aT_ready, 2 * G_ + 1)
                ps, free = ring(at, "t1", (dg,))
                evac(tT[:, :], ps[:, 0:T], free, tT_ready, 2 * G_ + 1)

            def shift1(at, G_, dg):
                ps, free = ring(at, "xT", (dg,))
                evac(xT[:, :], ps[:, 0:T], free, aT_ready, 2 * G_ + 2)
                ps, free = ring(at, "t2", (dg,))
                act.wait_ge(tm_ready, 2 * GRP * G_ + GRP)
                evac(tT[:, :], ps[:, 0:T], free, tT_ready, 2 * G_ + 2)

            def first_exp(at, G_, dg, i):
                ps, free = ring(at, "first_exp", (dg, i))
                act.activation(P1[:, i % 2, :, :].rearrange("p a b -> p (a b)"), ps[0:HT, 0:2 * T], ACT.Exp,
                               scale=float(D) ** -0.5).then_inc(P1_ready, 1)
                act.wait_ge(P1_ready, GRP * G_ + i + 1)
                act.sem_inc(free, 1)

            def stream(at, G_, dg, q):
                ps, free = ring(at, "uT", (dg, q))
                evac(uT[:, :], ps[:, 0:T], free, uT_ready, 2 * G_ + q + 1)
                ps, free = ring(at, "zT", (dg, q))
                evac(zT[:, q, :], ps[:, 0:T], free, zT_ready, 2 * G_ + q + 1)

            def gates(at, G_, dg):
                act.wait_ge(gates_in, G_ + 1)
                act.activation(soft[:, 1, :], soft[:, 0, :], ACT.Exp).then_inc(gates_exp, 1)

            def turn_u(at, G_, dg, i):
                ps, free = ring(at, "turn_u", (dg, i))
                evac(UT[:, i, :], ps[0:U, 0:T], free, UT_ready, GRP * G_ + i + 1)

            def hidden(at, G_, dg, i):
                for b in range(NF // 2):
                    ps, free = ring(at, "hid", (dg, i, b))
                    act.activation(hid[:, i, 2 * b:2 * b + 2, :].rearrange("p a b -> p (a b)"),
                                   ps[:, 0:2 * T], ACT.Gelu).then_inc(free, 1)

            def project(at, G_, dg, i):
                n_ = GRP * G_ + i
                act.wait_ge(qk_out, 16 * n_ + ONE)
                for m in range(2):
                    slot, k = at.uses(("qk"[m], (dg, i)))
                    act.wait_ge(misc_full[slot], k + 1)
                    act.copy(qk16[:, m, 0, :, :].rearrange("p c t -> p (c t)"), misc_ps[slot][0:DC, 0:2 * T]) \
                        .then_inc(hi_ready, 1)

            def shift(at, G_, dg, i, part):
                n_ = GRP * G_ + i
                ps, free = ring(at, "shift", (dg, i, part))
                act.wait_ge(shift_in[part], 16 * n_ + ONE)
                evac(shiftT[:, part, :], ps[0:6, 0:T], free, shift_ready, 2 * n_ + part + 1)

            def score(at, G_, dg, i, h):
                s = h % 2
                n_ = GRP * G_ + i
                act.wait_ge(score_full[s], 6 * n_ + h // 2 + 1)
                act.wait_ge(probs_used[h % NP], 3 * n_ + h // NP + ONE)
                act.activation(Pb[:, h % NP, :, :].rearrange("p a b -> p (a b)"), score_ps[s][0:HT, 0:2 * T],
                               ACT.Exp, scale=float(DH) ** -0.5).then_inc(score_free[s], 1)

            def mix(at, G_, dg, i, h):
                if h % 4 == 3:
                    c = h // 4
                    n_ = GRP * G_ + i
                    ps, free = ring(at, "O", (dg, i, c))
                    act.wait_ge(onT_ready, 3 * n_ + c + ONE)
                    evac(oT[:, c, :], ps[:, 0:T], free, oT_ready, 3 * n_ + c + 1)

            run(act, {"load": load, "tokens": tokens, "norm1": norm1, "shift1": shift1,
                      "first_exp": first_exp, "stream": stream, "gates": gates, "turn_u": turn_u,
                      "hidden": hidden, "project": project, "shift": shift, "score": score, "mix": mix})

        @block.vector
        def _(dve):
            dve.memset(qs[:, :, :, :], 0.0)
            dve.memset(vals[:, :, :, :, :], 1.0)
            dve.memset(z_tok[:, :, :, :], 0.0)
            dve.memset(a_tok[:, :, :, :], 0.0).then_inc(zeroed_dve, 1)
            dve.wait_ge(zeroed_dve, 1)
            dve.memset(a_tok[:, :, :, 12:14], 1.0)
            dve.memset(zs[:, :, :], 1.0)
            dve.memset(A_rep[:, :, :], 0.0)
            dve.memset(S_rep[:, :], 0.0)
            for s in range(MISC):
                pass
            dve.memset(w2_pad, 0.0).then_inc(zeroed_dve, 1)
            dve.wait_ge(zeroed_dve, 2)
            dve.wait_ge(w_in, 16 * W_LOADS)
            dve.wait_ge(cst_in, 16)
            k = 2

            def done(ins):
                nonlocal k
                k += 1
                ins.then_inc(zeroed_dve, 1)
                dve.wait_ge(zeroed_dve, k)

            done(dve.tensor_reduce(mean[0:C, 0:1], cw_in[:, :], AX.X, ALU.add))
            done(dve.tensor_scalar(mean[0:C, 1:2], mean[0:C, 0:1], 1.0 / D, None, ALU.mult))
            dve.tensor_scalar(cwc[:, :], cw_in[:, :], mean[0:C, 1:2], None, ALU.subtract).then_inc(su_dve, 1)
            done(dve.tensor_tensor(w2_pad[:, :, 0:HID], w2_in[:, 0:2, 0:HID], w2_in[:, 2:4, 0:HID], ALU.add))
            for o in range(2):
                last = dve.tensor_tensor(
                    w2_pad[:, o, HID:].rearrange("p (h w) -> p h w", w=32)[:, :, 0:DH],
                    w2_in[:, o, HID:].rearrange("p (h w) -> p h w", w=DH),
                    w2_in[:, 2 + o, HID:].rearrange("p (h w) -> p h w", w=DH), ALU.add)
            last.then_inc(su_dve, 1)
            dve.tensor_tensor(b2_in[:, 2, :], b2_in[:, 0, :], b2_in[:, 1, :], ALU.add).then_inc(su_dve, 1)
            dve.memset(peaks[:, :, :, :], 0.0).then_inc(su_dve, 1)
            dve.wait_ge(su_dma, 16)
            done(dve.tensor_reduce(mean[:, 0:1], G, AX.X, ALU.add))
            done(dve.tensor_scalar(mean[:, 1:2], mean[:, 0:1], 1.0 / D, None, ALU.mult))
            dve.tensor_scalar(Gc, G, mean[:, 1:2], None, ALU.subtract).then_inc(su_dve, 1)
            dve.wait_ge(su_pe, 5)
            dve.tensor_copy(A_rep[:, :, 0:13], banks[2][0:13, 0:13].unsqueeze(1).broadcast_to([13, 8, 13]))
            dve.tensor_scalar(S_rep[:, 0:128].rearrange("p (a b) -> p a b", a=4)[:, :, 0:Z],
                              banks[3][0:Z, 0:Z].unsqueeze(1).broadcast_to([Z, 4, Z]), 1.0 / D, None, ALU.mult)
            dve.tensor_scalar(S12[:, :].rearrange("p (a b) -> p a b", a=2),
                              banks[3][0:C, 0:C].unsqueeze(1).broadcast_to([C, 2, C]), 1.0 / D, None, ALU.mult)
            dve.tensor_copy(S_rep[:, 128:148].rearrange("p (a b) -> p a b", a=4)[:, :, 0:E],
                            banks[0][0:Z, 64:64 + E].unsqueeze(1).broadcast_to([Z, 4, E]))
            dve.tensor_copy(S_rep[:, 128:148].rearrange("p (a b) -> p a b", a=4)[:, :, E:E + 1],
                            mean[:, 1:2].unsqueeze(1).broadcast_to([Z, 4, 1])).then_inc(su_dve, 1)
            dve.wait_ge(turn_free, NT)
            for c in range(2):
                dve.tensor_scalar(GgT[:, c, 0:Z], GcT[:, c, :], gb[:, 0, c:c + 1], None, ALU.mult)
                done(dve.tensor_copy(GgT[:, c, Z:ZS], gb[:, 1, c:c + 1]))
                last = dve.tensor_tensor(L[:, c, :, :], GgT[:, c, :].unsqueeze(1).broadcast_to([DC, E, ZS]),
                                         const("emask", DC)[:, E * c:E * c + E].unsqueeze(2)
                                         .broadcast_to([DC, E, ZS]), ALU.mult)
            last.then_inc(su_dve, 1)
            dve.wait_ge(su_pe, 9)
            done(dve.tensor_tensor(Abd[:, 0, :], banks[1][:, 0:128], const("mask8"), ALU.mult))
            dve.tensor_tensor(Abd[:, 1, :], Abd[:, 0, :], const("one13"), ALU.add)
            dve.tensor_tensor(WR[:, :], banks[2][:, 128:276], const("mask4"), ALU.mult)
            for j in range(QUAD):
                dve.tensor_scalar(G4[:, j, :], banks[3][:, 128:128 + D], const("col4")[:, j:j + 1], None,
                                  ALU.mult)
            dve.tensor_tensor(WI[:, 0:24], banks[0][0:24, 128:152], const("mask2", 24), ALU.mult)
            dve.tensor_copy(WI[:, 24:48], ident[0:24, 0:24]).then_inc(su_dve, 1)

            def ring(at, *key):
                slot, k_ = at.uses(key)
                dve.wait_ge(misc_full[slot], k_ + 1)
                return misc_ps[slot], misc_free[slot]

            state = [0]

            def chain(at, ins):
                state[0] += 1
                ins.then_inc(link, 1)
                dve.wait_ge(link, at.link_at(state[0]))

            def linked(op, count):
                assert state[0] == count, (op, state[0])
                state[0] = 0

            def pool(at, G_, dg, m):
                for t in range(TILES):
                    n_ = TILES * m + t
                    dve.wait_ge(x_in[n_ % NX], 16 * (TILES * (GRP // PAIR) // NX * G_ + n_ // NX + 1))
                    if m >= 2 or True:
                        dve.wait_ge(masked, 4 * G_ + (m - 1 if m else 0))
                    v = xt[:, n_ % NX, :].rearrange("p (k j w) -> p j k w", k=PATCH, w=PATCH)
                    for j in range(0, GRID, 2):
                        last = dve.tensor_reduce(psums[:, m % 2, t, j:j + 2], v[:, j:j + 2, :, :], AX.XY, ALU.add)
                    last.then_inc(pooled, 1)

            def tokens(at, G_, dg, m):
                ps, free = ring(at, "tok", (dg, m))
                v = ps[0:HT, 0:96].rearrange("p (h w b c) -> p h w b c", h=2, w=2, b=PAIR)
                dve.tensor_copy(wtok[:, :, PAIR * m:PAIR * m + PAIR, :], v[:, :, 0, :, :])
                dve.tensor_copy(z_tok[:, :, PAIR * m:PAIR * m + PAIR, 0:C], v[:, :, 1, :, :]).then_inc(free, 1)
                if m == GRP // PAIR - 1:
                    slot, k_ = at.uses(("tok", (dg, m)))
                    dve.wait_ge(misc_free[slot], k_ + 1)

            def norm1(at, G_, dg):
                t12 = tmp[:, :, :, 0:C].rearrange("p h i c -> p (h i) c")
                chain(at, dve.tensor_tensor(t12, z_tok[:, :, :, 0:C].rearrange("p h i c -> p (h i) c"),
                                            wtok[:, :, :, :].rearrange("p h i c -> p (h i) c"), ALU.mult))
                chain(at, dve.tensor_reduce(var[:, 0, :], t12, AX.X, ALU.add))
                dve.tensor_scalar(var[:, 1, :], var[:, 0, :], 1e-5, None, ALU.add).then_inc(dve_pow, 1)
                dve.wait_ge(gp_pow, 3 * G_ + 1)
                chain(at, dve.tensor_tensor(
                    a_tok[:, :, :, 0:C].rearrange("p h i c -> p (h i) c"),
                    z_tok[:, :, :, 0:C].rearrange("p h i c -> p (h i) c"),
                    var[:, 2, :].unsqueeze(2).broadcast_to([HT, 2 * GRP, C]), ALU.mult))
                dve.tensor_copy(x_tok[:, :, :, :], a_tok[:, :, :, 0:16]).then_inc(a_ready, 1)
                linked("norm1", 3)

            def first_max(at, G_, dg, i):
                ps, free = ring(at, "first_max", (dg, i))
                dve.tensor_reduce(nm1[:, :, i], ps[0:HT, 0:2 * T].rearrange("p (h k) -> p h k", h=2),
                                  AX.X, ALU.max, negate=True).then_inc(free, 1)

            def shift1(at, G_, dg):
                slot, k_ = at.uses(("first_max", (dg, GRP - 1)))
                dve.wait_ge(misc_free[slot], k_ + 1)
                dve.wait_ge(a_ready, G_ + 1)
                chain(at, dve.engine_nop() if False else
                      dve.tensor_copy(x_tok[:, :, :, 13], nm1[:, :, :]))
                chain(at, dve.tensor_copy(x_tok[:, :, :, 12], a_tok[:, :, :, 12]))
                dve.sem_inc(x_ready, 1)
                linked("shift1", 2)

            def stream(at, G_, dg, q):
                i = QUAD * q
                ps, free = ring(at, "utok", (dg, q))
                v = ps[0:HT, 0:256].rearrange("p (h i c) -> p h i c", h=2, i=QUAD)
                chain(at, dve.reciprocal(urec[:, :, :], v[:, :, :, 12]))
                for h in range(2):
                    last = dve.tensor_tensor(z_tok[:, h, i:i + QUAD, C:Z], v[:, h, :, 0:13],
                                             urec[:, h, :].unsqueeze(2).broadcast_to([HT, QUAD, 13]), ALU.mult)
                last.then_inc(z_ready, 1)
                dve.wait_ge(z_ready, 2 * G_ + q + 1)
                dve.sem_inc(free, 1)
                ps, free = ring(at, "w2", (dg, q))
                v = ps[0:HT, 0:296].rearrange("p (h w) -> p h w", h=2)
                for h in range(2):
                    last = dve.tensor_tensor(tmp[:, h, i:i + QUAD, 0:Z],
                                             v[:, h, 0:128].rearrange("p (i c) -> p i c", i=QUAD)[:, :, 0:Z],
                                             z_tok[:, h, i:i + QUAD, 0:Z], ALU.mult)
                chain(at, last)
                chain(at, dve.tensor_reduce(var[:, 3, :].rearrange("p (h i) -> p h i", h=2)[:, :, i:i + QUAD],
                                            tmp[:, :, i:i + QUAD, 0:Z], AX.X, ALU.add))
                for h in range(2):
                    last = dve.tensor_copy(lg[:, h, i:i + QUAD, :],
                                           v[:, h, 128:148].rearrange("p (i e) -> p i e", i=QUAD))
                last.then_inc(free, 1)
                if q == 1:
                    slot, k_ = at.uses(("w2", (dg, q)))
                    dve.wait_ge(misc_free[slot], k_ + 1)
                linked("stream", 3)

            def gates(at, G_, dg):
                lgv = lg[:, :, :, :].rearrange("p h i e -> p (h i) e")
                s0 = soft[:, 0, :].rearrange("p (n e) -> p n e", e=E)
                s1 = soft[:, 1, :].rearrange("p (n e) -> p n e", e=E)
                s2 = soft[:, 2, :].rearrange("p (n e) -> p n e", e=E)

                def wide(a):
                    return a.unsqueeze(2).broadcast_to([HT, 2 * GRP, E])

                dve.tensor_scalar(var[:, 1, :], var[:, 3, :], 1e-5, None, ALU.add).then_inc(dve_pow, 1)
                dve.wait_ge(gp_pow, 3 * G_ + 2)
                chain(at, dve.tensor_tensor(s2, lgv[:, :, 0:E], wide(var[:, 2, :]), ALU.mult))
                chain(at, dve.tensor_reduce(red[:, 0, :], s2, AX.X, ALU.max))
                chain(at, dve.tensor_tensor(s0, s2, wide(red[:, 0, :]), ALU.subtract))
                dve.sem_inc(gates_in, 1)
                dve.tensor_copy(var[:, 6, :], var[:, 2, :])
                chain(at, dve.tensor_tensor(var[:, 4, :], var[:, 2, :], var[:, 2, :], ALU.mult))
                chain(at, dve.tensor_tensor(var[:, 5, :], var[:, 4, :], var[:, 3, :], ALU.mult))
                dve.tensor_scalar(var[:, 1, :], var[:, 5, :], 1e-6, None, ALU.add).then_inc(dve_pow, 1)
                dve.wait_ge(gp_pow, 3 * G_ + 3)
                chain(at, dve.tensor_tensor(var[:, 7, :], var[:, 6, :], var[:, 2, :], ALU.mult))
                chain(at, dve.tensor_scalar(var[:, 5, :], var[:, 6, :], 1.0, None, ALU.add))
                dve.wait_ge(gates_exp, G_ + 1)
                chain(at, dve.tensor_reduce(red[:, 1, :], s1, AX.X, ALU.add))
                chain(at, dve.reciprocal(red[:, 2, :], red[:, 1, :]))
                pr = prob[:, :, :].rearrange("p h (i e) -> p (h i) e", e=E)
                chain(at, dve.tensor_tensor(pr, s1, wide(red[:, 2, :]), ALU.mult))
                dve.sem_inc(prob_ready, 1)
                ps, free = ring(at, "gates", (dg,))
                chain(at, dve.tensor_copy(rows[:, :], ps[0:GRP * E, 0:T]))
                dve.sem_inc(free, 1)
                linked("gates", 11)

            def choose(at, G_, dg, part):
                for r in range(CHOOSE[part]):
                    settled(dve)
                    chain(at, dve.max(top8[:, :], rows[:, :]))
                    if part == 2 and r == CHOOSE[2] - 1:
                        chain(at, dve.memset(top8[:, CAP % 8:8], REPLACED))
                    settled(dve)
                    chain(at, dve.match_replace(rows[:, :], top8[:, :], rows[:, :], REPLACED))
                if part == 2:
                    chain(at, dve.tensor_scalar(rows[:, :], rows[:, :], 0.0, None, ALU.is_lt))
                    dve.sem_inc(sel_rows, 1)
                linked("choose", link_count(("choose", 0, part)))

            def chosen(at, G_, dg):
                ps, free = ring(at, "chosen", (dg,))
                dve.tensor_copy(sel[:, :, :].rearrange("p h w -> p (h w)"), ps[0:HT, 0:64]).then_inc(sel_ready, 1)
                dve.wait_ge(sel_ready, G_ + 1)
                dve.sem_inc(free, 1)

            def spread(at, G_, dg):
                sv = sel[:, :, :].rearrange("p h (i e) -> p (h i) e", e=E)
                pv = prob[:, :, :].rearrange("p h (i e) -> p (h i) e", e=E)
                n_ = 2 * GRP
                dve.wait_ge(sel_ready, G_ + 1)
                dve.wait_ge(gated, GRP * G_ + ONE)
                chain(at, dve.tensor_tensor(cg[:, :, :], sv, pv, ALU.mult))
                chain(at, dve.tensor_copy(gate8[:, :, 4:8], cg[:, :, 3:4].broadcast_to([HT, n_, 4])))
                chain(at, dve.tensor_tensor(gate8[:, :, 2:4], cg[:, :, 2:3].broadcast_to([HT, n_, 2]),
                                            gate8[:, :, 4:6], ALU.add))
                chain(at, dve.tensor_tensor(gate8[:, :, 1:2], cg[:, :, 1:2], gate8[:, :, 2:3], ALU.add))
                chain(at, dve.tensor_tensor(gate8[:, :, 0:1], cg[:, :, 0:1], gate8[:, :, 1:2], ALU.add))
                chain(at, dve.tensor_tensor(zs[:, :, 0:Z], z_tok[:, :, :, 0:Z].rearrange("p h i c -> p (h i) c"),
                                            var[:, 7, :].unsqueeze(2).broadcast_to([HT, n_, Z]), ALU.mult))
                for e in range(E):
                    last = dve.tensor_tensor(u_tok[:, :, e, :], zs[:, :, :],
                                             sv[:, :, e:e + 1].broadcast_to([HT, n_, ZS]), ALU.mult)
                last.then_inc(u_ready, 1)
                linked("spread", 6)

            def residual(at, G_, dg, i):
                ps, free = ring(at, "residual", (dg, i))
                if i == 0:
                    dve.wait_ge(fin_ready, GRP * G_ + ONE)
                for h in range(2):
                    last = dve.tensor_scalar(resid[:, i, h, :], ps[0:HT, D * h:D * h + D],
                                             var[:, 5, GRP * h + i:GRP * h + i + 1], lg[:, h, i, 4:5],
                                             ALU.mult, ALU.add)
                last.then_inc(free, 1)
                if i == GRP - 1:
                    slot, k_ = at.uses(("residual", (dg, i)))
                    dve.wait_ge(misc_free[slot], k_ + 1)
                    dve.sem_inc(resid_ready, 1)

            def project(at, G_, dg, i):
                for m in range(2):
                    slot, k_ = at.uses(("qk"[m], (dg, i)))
                    n_ = 2 * (GRP * G_ + i) + m + 1
                    dve.wait_ge(hi_ready, n_)
                    dve.tensor_tensor(qk16[:, m, 1, :, :].rearrange("p c t -> p (c t)"),
                                      misc_ps[slot][0:DC, 0:2 * T],
                                      qk16[:, m, 0, :, :].rearrange("p c t -> p (c t)"),
                                      ALU.subtract).then_inc(lo_ready, 1)
                    dve.wait_ge(lo_ready, n_)
                    dve.sem_inc(misc_free[slot], 1)

            def values(at, G_, dg, i):
                ps, free = ring(at, "values", (dg, i))
                for h in range(2):
                    last = dve.tensor_copy(vals[:, i % 2, h, :, 0:DH],
                                           ps[0:HT, D * h:D * h + D].rearrange("p (h d) -> p h d", d=DH))
                last.then_inc(vals_ready, 1)
                dve.wait_ge(vals_ready, GRP * G_ + i + 1)
                dve.sem_inc(free, 1)

            def peak(at, G_, dg, i, h):
                s = h % 2
                n_ = 6 * (GRP * G_ + i) + h // 2 + 1
                dve.wait_ge(peak_full[s], n_)
                dve.tensor_reduce(peaks[:, h // 6, :, h % 6],
                                  peak_ps[s][0:HT, 0:2 * T].rearrange("p (q k) -> p q k", q=2),
                                  AX.X, ALU.max, negate=True).then_inc(peak_free[s], 1)
                if h % 6 == 5:
                    dve.wait_ge(peak_free[s], n_ + ONE)
                    dve.sem_inc(peaks_ready, 1)

            def norm(at, G_, dg, i, c):
                n_ = 3 * (GRP * G_ + i) + c
                ps, free = ring(at, "den", (dg, i, c))
                dve.wait_ge(onT_ready, n_ + ONE)
                dve.reciprocal(rden[:, c, :], ps[:, 0:T]).then_inc(rden_ready, 1)
                dve.wait_ge(rden_ready, n_ + 1)
                dve.sem_inc(free, 1)

            def fc2(at, G_, dg, i, k_):
                if k_ == 3:
                    n_ = GRP * G_ + i
                    ps, free = ring(at, "B", (dg, i))
                    dve.wait_ge(out_done[i % 2], 16 * (GRP // 2 * G_ + i // 2) + ONE)
                    for h in range(2):
                        last = dve.tensor_tensor(
                            fin[:, i % 2, h, :].rearrange("p (s w) -> p s w", s=8),
                            ps[0:HT, D * h:D * h + D].rearrange("p (s w) -> p s w", s=8),
                            gate8[:, GRP * h + i, :].unsqueeze(2).broadcast_to([HT, 8, D // 8]), ALU.mult)
                    last.then_inc(gated, 1)
                    dve.wait_ge(gated, n_ + 1 + ONE)
                    dve.sem_inc(free, 1)

            run(dve, {"pool": pool, "tokens": tokens, "norm1": norm1, "first_max": first_max,
                      "shift1": shift1, "stream": stream, "gates": gates, "choose": choose,
                      "chosen": chosen, "spread": spread, "residual": residual, "project": project,
                      "values": values, "peak": peak, "norm": norm, "fc2": fc2})

        @block.gpsimd
        def _(pool_e):
            gp = pool_e
            gp.memset(ks[:, :, :, :], 0.0).then_inc(gp_in, 1)
            gp.wait_ge(gp_in, 1)
            gp.memset(ks[KS:KS + 1, :, :, :], 1.0).then_inc(zeroed, 1)
            gp.wait_ge(zeroed, 1)
            gp.wait_ge(cst_in, 16)

            def pool(at, G_, dg, m):
                gp.wait_ge(planes_out, 4 * G_ + m)
                for t in range(TILES):
                    gp.wait_ge(pooled, 12 * G_ + TILES * m + t + 1)
                    last = gp.tensor_tensor(
                        spread_p[:, t, :, :],
                        psums[:, m % 2, t, :].unsqueeze(1).broadcast_to([PP, GRID, GRID]),
                        const("rowsel", PP).unsqueeze(2).broadcast_to([PP, GRID, GRID]), ALU.mult)
                last.then_inc(masked, 1)

            def rsqrt(G_, n_):
                gp.wait_ge(dve_pow, 3 * G_ + n_)
                gp.tensor_tensor(var[:, 2, :], var[:, 1, :], const("half", HT), ALU.pow).then_inc(gp_pow, 1)

            def norm1(at, G_, dg):
                rsqrt(G_, 1)

            def gates(at, G_, dg):
                rsqrt(G_, 2)
                rsqrt(G_, 3)

            def mask_image(at, G_, dg, i, second):
                if i == 0:
                    gp.wait_ge(tT_ready, 2 * G_ + second + 1)
                if i >= 2:
                    slot, k_ = at.uses((("first_max", "first_exp")[second], (dg, i - 2)))
                    gp.wait_ge(misc_full[slot], k_ + 1)
                settled(gp)
                gp.tensor_scalar(tm[:, i % 2, :], tT[:, :], const("col8")[:, i:i + 1], 1.0, ALU.mult, ALU.mult) \
                    .then_inc(tm_ready, 1)

            def first_max(at, G_, dg, i):
                mask_image(at, G_, dg, i, 0)

            def first_exp(at, G_, dg, i):
                mask_image(at, G_, dg, i, 1)

            def norm(at, G_, dg, i, c):
                n_ = 3 * (GRP * G_ + i) + c
                gp.wait_ge(rden_ready, n_ + 1)
                gp.wait_ge(gated, GRP * G_ + i + ONE)
                gp.tensor_tensor(onT[:, c, :], oT[:, c, :], rden[:, c, :], ALU.mult).then_inc(onT_ready, 1)

            def fc2(at, G_, dg, i, k_):
                if k_ == 3:
                    n_ = GRP * G_ + i
                    gp.wait_ge(gated, n_ + 1 + ONE)
                    gp.wait_ge(resid_ready, G_ + 1)
                    gp.tensor_tensor(fin[:, i % 2, :, :], fin[:, i % 2, :, :], resid[:, i, :, :], ALU.add) \
                        .then_inc(fin_ready, 1)

            run(gp, {"pool": pool, "norm1": norm1, "gates": gates, "first_max": first_max,
                     "first_exp": first_exp, "norm": norm, "fc2": fc2})


_INS = ["x", "L0_tok_channel_weights", "L0_attn_Wq", "L0_attn_bq", "L0_attn_Wk", "L0_attn_bk", "L0_attn_Wv",
        "L0_attn_bv", "L0_ffn_w_router", "L0_ffn_gamma1", "L0_ffn_beta1", "L0_ffn_w1", "L0_ffn_b1",
        "L0_ffn_w2", "L0_ffn_b2"]


def kernel(**inputs):
    import concourse.bacc as _bacc
    from concourse.bass_utils import run_bass_kernel_spmd as _run

    nc = _bacc.Bacc("TRN2", target_bir_lowering=False, num_devices=1)
    arrays, args = {}, []
    for name in _INS:
        a = np.ascontiguousarray(inputs[name])
        arrays[f"in_{name}_dram"] = a
        args.append(nc.dram_tensor(f"in_{name}_dram", a.shape, mybir.dt.from_np(a.dtype), kind="ExternalInput").ap())
    arrays["in_consts_dram"] = constants()
    args.append(nc.dram_tensor("in_consts_dram", (128, NCONST), F32, kind="ExternalInput").ap())
    shape = (inputs["x"].shape[0], T, D)
    args.append(nc.dram_tensor("out_0_dram", shape, F32, kind="ExternalOutput").ap())
    bass_vit_tower(nc, *args)
    r = _run(nc, [arrays], core_ids=[0])
    return r.results[0]["out_0_dram"]
```

```python
from contextlib import ExitStack

import numpy as np

import concourse.bass as bass
from concourse import mybir

ALU = mybir.AluOpType
ACT = mybir.ActivationFunctionType
AX = mybir.AxisListType
F32 = mybir.dt.float32
F16 = mybir.dt.float16

C, SIDE, PATCH = 12, 224, 16
GRID = SIDE // PATCH
T = GRID * GRID
HT = T // 2
D = 192
DC = D // 2
E = 4
CAP = T // 2
H, DH = 12, 16
HID = 4 * D
F1 = HID + 3 * D
NF = HID // 128
Z = 2 * C + 1
ZS = Z + 1
U = E * ZS
GRP = 8
QUAD = 4
PAIR = 2
TILES = 3
PLANES = PAIR * C // TILES
PP = PLANES * GRID
XROW = PATCH * SIDE
NX = 3
NSTACK = 4
KS = 96
MISC = 4
ONE = 1
W_LOADS = 20
NP = 4
NRES = 4
REPLACED = -1.0

CONST = {}
_at = 0
for _name, _w in (("ident", 128), ("plane", TILES * PAIR * C), ("den", 128), ("mask8", 128), ("one13", 128),
                  ("mask4", 4 * 32 + 4 * 5), ("col8", GRP), ("col4", QUAD), ("rep25", 128), ("rep13", 128),
                  ("rep12", 24), ("mask2", 24), ("emask", 2 * E), ("last", U), ("rowsel", GRID), ("half", 16)):
    CONST[_name] = (_at, _w)
    _at += _w
NCONST = _at


def constants():
    c = np.zeros((128, NCONST), np.float32)

    def put(name, a):
        a = np.asarray(a, np.float32)
        at, w = CONST[name]
        c[: a.shape[0], at:at + w] = a.reshape(a.shape[0], w)

    p, q = np.arange(128)[:, None], np.arange(128)[None, :]
    put("ident", p == q)
    plane = np.zeros((PP, TILES, PAIR * C))
    for t in range(TILES):
        for r in range(PP):
            plane[r, t, t * PLANES + r // GRID] = 1
    put("plane", plane)
    put("den", (p // 32 == q // 32) & (p % 32 == DH))
    put("mask8", p // 16 == q // 16)
    put("one13", (p == q) & (p % 16 == 13))
    j = np.arange(148)[None, :]
    put("mask4", np.where(j < 128, p // 32 == j // 32, p // 32 == (j - 128) // 5))
    put("col8", p // 16 == np.arange(GRP)[None, :])
    put("col4", p // 32 == np.arange(QUAD)[None, :])
    put("rep25", (q % 32 == p)[:Z])
    put("rep13", (q % 16 == p)[:13])
    k = np.arange(24)
    put("rep12", (k[None, :] % 12 == np.arange(12)[:, None]))
    put("mask2", k[None, :] // 12 == k[:, None] // 12)
    d = np.arange(DC)[:, None, None] + DC * np.arange(2)[None, :, None]
    put("emask", d < (D >> (E - 1 - np.arange(E)))[None, None, :])
    put("last", (np.arange(U) % ZS == Z)[None, :])
    put("rowsel", p[:PP] % GRID == np.arange(GRID)[None, :])
    put("half", np.full((128, 16), -0.5))
    return c



PIECES = GRID // 2
ROUNDS = -(-CAP // 8)
EARLY = 5
FC2 = 6


def front():
    ops = []
    n = 0
    for m in range(GRP // PAIR):
        for t in range(TILES):
            for p in range(PIECES):
                slot = n // EARLY - GRP if n < EARLY * GRP else n - EARLY * GRP
                ops.append((slot, ("pool", m, t, p)))
                n += 1
            ops.append((slot + (1 if slot < 0 else 0.5), ("own_row", m, t)))
            if TILES * m + t + NX < TILES * GRP // PAIR:
                ops.append((slot + (1 if slot < 0 else 0.5), ("fetch", m, t)))
        later = 1 if slot < 0 else 2
        ops.append((slot + later, ("planes", m)))
        ops.append((slot + later + 1, ("tok", m)))
    at = slot + 4
    ops += [(at, ("norm1_scale",)), (at + 2, ("norm1",)), (at + 3, ("norm1_turn",)), (at + 4, ("norm1_key",)),
            (at + 5, ("own_image", 0, 0))]
    at += 6
    for i in range(GRP):
        if i + 1 < GRP:
            ops.append((at + 1.3 * i, ("own_image", i + 1, 0)))
        ops.append((at + 1.3 * i, ("first_max", i)))
    at += 1.3 * GRP
    ops += [(at, ("shift1",)), (at + 1, ("shift1_turn",)), (at + 2, ("shift1_key",)), (at + 3, ("own_image", 0, 1))]
    at += 4
    for i in range(GRP):
        if i + 1 < GRP:
            ops.append((at + i, ("own_image", i + 1, 1)))
        ops.append((at + i, ("first_exp", i)))
        ops.append((at + i + 1.5, ("first_mix", i)))
    for q in range(GRP // QUAD):
        for k, name in enumerate(("stream_sum", "stream", "stream_turn", "stream_norm")):
            ops.append((at + 2 + 4 * q + QUAD - 0.2 + k, (name, q)))
    at += 14
    ops += [(at, ("gate_scale",)), (at + 1, ("gate_logits",)), (at + 3, ("gates",)), (at + 4, ("gate_rows",))]
    for r in range(ROUNDS):
        ops.append((at + 5 + 0.5 * r, ("choose", r)))
    at += 5 + 0.5 * ROUNDS
    ops += [(at + 0.5, ("chosen",)), (at + 1, ("spread",))]
    return sorted(ops, key=lambda o: o[0])


def turn(dg):
    ops = [("turn_u", dg, 0), ("turn_u", dg, 1), ("project", dg, 0)]
    return ops + [("turn_u", dg, i) for i in range(2, GRP)] + [("project", dg, 1)]


def body(with_next):
    ops = []
    slots = {s: [] for s in range(-GRP, H * GRP)}
    if with_next:
        for slot, op in front():
            slots[min(int(np.floor(slot)), H * GRP - 1)].append((op[0], 1) + op[1:])
        ops.append(("load", 1))
    ops.append(("gate8", 0))
    for i in range(GRP):
        ops.append(("hidden", 0, i))
        if i == 0:
            ops.append(("values", 0, 0))
        heads = range(3 * (i - 2), 3 * (i - 2) + 3) if 2 <= i < 6 else ()
        for h in heads:
            ops.append(("peak", 0, 0, h))
        ops += slots[i - GRP]
        if i == 4:
            ops.append(("shift", 0, 0, 0))
        if i == 6:
            ops.append(("shift", 0, 0, 1))
        if i < NRES:
            ops.append(("residual", 0, i))
    for i in range(GRP):
        fill = [slots[H * i + h] for h in range(H)]
        if i:
            fill[0] = [("shift", 0, i, 1)] + fill[0] if i else fill[0]
            fill[1] = [("norm", 0, i - 1, 2)] + fill[1]
            for k in range(FC2):
                fill[2 + k] = [("fc2", 0, i - 1, k)] + fill[2 + k]
            if i - 1 + NRES < GRP:
                fill[9] = fill[9] + [("residual", 0, i - 1 + NRES)]
        fill[8] = fill[8] + [("norm", 0, i, 0)]
        fill[10] = fill[10] + [("norm", 0, i, 1)]
        if i + 1 < GRP:
            fill[7] = [("shift", 0, i + 1, 0)] + fill[7]
            fill[10] = [("values", 0, i + 1)] + fill[10]
        if i + 2 < GRP:
            fill[1] = [("project", 0, i + 2)] + fill[1]
        for h in range(H):
            if i + 1 < GRP:
                ops.append(("peak", 0, i + 1, h))
            ops.append(("score", 0, i, h))
            ops += fill[h]
            if h:
                ops.append(("mix", 0, i, h - 1))
        ops.append(("mix", 0, i, H - 1))
    rest = turn(1) if with_next else []
    ops += rest[:2]
    ops.append(("norm", 0, GRP - 1, 2))
    ops += rest[2:5] 
    for k in range(FC2):
        ops.append(("fc2", 0, GRP - 1, k))
    ops += rest[5:]
    return ops


def ring_of(op):
    name, key = op[0], op[1:]
    if name == "first_mix":
        g, i = key
        k = [("uT", (g, i // QUAD))]
        return (k if i % QUAD == 0 else []), []
    if name == "stream_sum":
        return [], [("uT", key)]
    if name == "hidden":
        ks = [("hid", key + (b,)) for b in range(NF // 2)]
        return ks, ks
    if name == "project":
        ks = [("q", key), ("k", key)]
        return ks, ks
    if name == "mix":
        g, i, h = key
        k = [("O", (g, i, h // 4))]
        return (k if h % 4 == 0 else []), (k if h % 4 == 3 else [])
    if name == "fc2":
        g, i, k = key
        ks = [("B", (g, i))]
        return (ks if k == 0 else []), (ks if k == FC2 - 1 else [])
    if name in ONE_BANK:
        return [(name, key)], [(name, key)]
    return [], []


ONE_BANK = {"planes", "tok", "norm1_turn", "norm1_key", "first_max", "shift1_turn", "shift1_key", "first_exp",
            "stream", "stream_turn", "stream_norm", "gate_rows", "chosen", "turn_u", "residual", "values",
            "shift", "norm"}


def plan_ring(ops):
    place, count, closed_at, open_ = {}, [0] * MISC, [-MISC + s for s in range(MISC)], set()
    for n, op in enumerate(ops):
        opens, closes = ring_of(op)
        for key in opens:
            free = [s for s in range(MISC) if s not in open_]
            slot = min(free, key=lambda s: closed_at[s])
            place[key] = (slot, count[slot])
            count[slot] += 1
            open_.add(slot)
            if key in closes:
                open_.discard(slot)
                closed_at[slot] = 10 * n + 10 + opens.index(key)
        for key in closes:
            if key not in opens:
                open_.discard(place[key][0])
                closed_at[place[key][0]] = 10 * n + 10
    return place, count


LINKS = {"norm1_scale": 2, "norm1": 1, "shift1": 2, "stream": 1, "stream_norm": 2, "gate_logits": 5,
         "gates": 5, "gate_rows": 1, "choose": 2, "spread": 1, "gate8": 5}


def link_count(op):
    if op[0] == "choose" and op[2] == ROUNDS - 1:
        return 4
    return LINKS.get(op[0], 0)


def bass_vit_tower(nc, x, cw, Wq, bq, Wk, bk, Wv, bv, w_router, gamma, beta, w1, b1, w2, b2, consts, out):
    B = x.shape[0]
    NG = B // GRP

    sections = {"pro": [], "loop": body(True), "last": body(False)}
    sections["pro"] = [("load", 0)] + [(op[0], 0) + op[1:] for _, op in front()] + turn(0)
    rings = {s: plan_ring(ops) for s, ops in sections.items()}
    links = {s: sum(link_count(op) for op in ops) for s, ops in sections.items()}

    ctx = ExitStack()
    with ctx:
        def sb(name, shape, dt=F32):
            return ctx.enter_context(nc.sbuf_tensor(name, shape, dt))

        def sem(name):
            return ctx.enter_context(nc.semaphore(name))

        cst = sb("cst", [128, NCONST])

        def const(name, rows=128):
            at, w = CONST[name]
            return cst[0:rows, at:at + w]

        ident = const("ident")

        xt = sb("xt", [PP, NX, XROW])
        psums = sb("psums", [PP, 2, TILES, GRID])
        spread_p = sb("spread_p", [PP, TILES, GRID, GRID])
        planesT = sb("planesT", [PAIR * C, T])
        wtok = sb("wtok", [HT, 2, GRP, C])
        tmp = sb("tmp", [HT, 2, GRP, 26])
        var = sb("var", [HT, 8, 2 * GRP])
        a_tok = sb("a_tok", [HT, 2, GRP, 32])
        x_tok = sb("x_tok", [HT, 2, GRP, 16])
        aT = sb("aT", [128, T])
        tT = sb("tT", [128, T])
        tm = sb("tm", [128, 2, T])
        nm1 = sb("nm1", [HT, 2, GRP])
        P1 = sb("P1", [HT, 2, 2, T])
        uT = sb("uT", [128, T])
        xT = uT
        urec = sb("urec", [HT, 2, QUAD])
        z_tok = sb("z_tok", [HT, 2, GRP, 32])
        zT = sb("zT", [128, GRP // QUAD, T])
        lg = sb("lg", [HT, 2, GRP, 5])
        soft = sb("soft", [HT, 3, 2 * GRP * E])
        red = sb("red", [HT, 3, 2 * GRP])
        prob = sb("prob", [HT, 2, GRP * E])
        rows = sb("rows", [GRP * E, T])
        top8 = sb("top8", [GRP * E, 8])
        sel = sb("sel", [HT, 2, GRP * E])
        cg = sb("cg", [HT, 2 * GRP, E])
        gate8 = sb("gate8", [HT, 2 * GRP, 8])
        zs = sb("zs", [HT, 2 * GRP, ZS])
        UT = sb("UT", [U, GRP, T])
        hid = sb("hid", [128, GRP, NF, T])
        qk16 = sb("qk16", [DC, 2, 2, 2, T], F16)
        qs = sb("qs", [KS + 1, NSTACK, H, T], F16)
        ks = sb("ks", [KS + 1, NSTACK, H, T], F16)
        vals = sb("vals", [HT, 2, 2, H, 32])
        peaks = sb("peaks", [HT, 2, 2, 6])
        shiftT = sb("shiftT", [6, 2, T], F16)
        Pb = sb("Pb", [HT, NP, 2, T])
        both = sb("both", [HT, NRES * 2 * D + 2 * GRP * U])
        resid = both[:, 0:NRES * 2 * D].rearrange("p (i h d) -> p i h d", i=NRES, h=2)
        u_tok = both[:, NRES * 2 * D:].rearrange("p (n e z) -> p n e z", n=2 * GRP, e=E)
        oT = sb("oT", [128, 3, T])
        rden = sb("rden", [128, 3, T])
        onT = sb("onT", [128, 3, T])
        fin = sb("fin", [HT, 2, 2, D])
        Abd = sb("Abd", [128, 2, 128])
        WR = sb("WR", [128, 148])
        G4 = sb("G4", [128, QUAD, D])
        WI = sb("WI", [2 * C, 48])
        M = sb("M", [U, F1])
        w2T = sb("w2T", [128, NF + 3, D])

        banks = [ctx.enter_context(nc.psum_tensor(f"bank{b}", [128, 512], F32)) for b in range(8)]
        score_ps = banks[0:2]
        peak_ps = banks[2:4]
        misc_ps = banks[4:8]
        qk_dram = nc.dram_tensor("qk_scratch", (2, 2, 2, 2, DC, T), F16, kind="Internal").ap()

        hflat = hid[:, :, :, :].rearrange("p a b c -> p (a b c)")
        n = 0

        def scratch(rows_, *shape):
            nonlocal n
            w = int(np.prod(shape))
            v = hflat[0:rows_, n:n + w]
            n += w
            if len(shape) == 2:
                v = v.rearrange("p (a b) -> p a b", a=shape[0])
            if len(shape) == 3:
                v = v.rearrange("p (a b c) -> p a b c", a=shape[0], b=shape[1])
            return v

        w1_in = scratch(128, 11, D)
        w2_in = scratch(DC, 4, HID + D)
        w1T = scratch(DC, 2, F1)
        G = scratch(Z, D)
        Gc = scratch(Z, D)
        Vp = scratch(C, D)
        w2_pad = both[0:DC, 0:2 * (HID + H * 32)] \
            .rearrange("p (o f) -> p o f", o=2)
        wa_in = Pb[0:DC, :, :, :].rearrange("p a b c -> p (a b c)")[:, 0:3 * 2 * D].rearrange("p (m o d) -> p m o d", m=3, o=2)
        wa_T = UT[0:DC, :, :].rearrange("p i t -> p (i t)")[:, 0:3 * 2 * D].rearrange("p (m o d) -> p m o d", m=3, o=2)
        early = tmp[0:C, :, :, :].rearrange("p a b c -> p (a b c)")
        cw_in = early[:, 0:D]
        cwc = early[:, D:2 * D]
        mean = sb("mean", [Z, 2])
        cwcT = sb("cwcT", [DC, 2, C])
        QKp = sb("QKp", [DC, 2, 2, 13])
        wr_in = wtok[0:E, :, :, :].rearrange("p a b c -> p (a b c)")
        RT = sb("RT", [DC, 2, E])
        GcT = sb("GcT", [DC, 2, Z])
        gb = sb("gb", [DC, 2, 2])
        GgT = sb("GgT", [DC, 2, ZS])
        L = P1[0:DC, :, :, :].rearrange("p a b c -> p (a b c)")[:, 0:2 * U].rearrange("p (c e z) -> p c e z", c=2, e=E)
        b1_in = M[0:1, :]
        b2_in = rden[0:1, :, :].rearrange("p a b -> p (a b)")[:, 0:3 * D].rearrange("p (a b) -> p a b", a=3)
        A_rep = sb("A_rep", [13, 8, 16])
        S_rep = soft[0:Z, :, :].rearrange("p a b -> p (a b)")[:, 0:148]
        S12 = sb("S12", [C, 24])

        w_in = sem("w_in")
        gp_in = sem("gp_in")
        cst_in = sem("cst_in")
        zeroed = sem("zeroed")
        zeroed_dve = sem("zeroed_dve")
        turn_full, turn_free = sem("turn_full"), sem("turn_free")
        su_dve, su_pe, su_act, su_dma = sem("su_dve"), sem("su_pe"), sem("su_act"), sem("su_dma")
        bias_in = sem("bias_in")
        misc_full = [sem(f"misc_full{s}") for s in range(MISC)]
        misc_free = [sem(f"misc_free{s}") for s in range(MISC)]
        peak_full = [sem(f"peak_full{s}") for s in range(2)]
        peak_free = [sem(f"peak_free{s}") for s in range(2)]
        score_full = [sem(f"score_full{s}") for s in range(2)]
        score_free = [sem(f"score_free{s}") for s in range(2)]
        probs_used = [sem(f"probs_used{s}") for s in range(NP)]
        x_in = [sem(f"x_in{s}") for s in range(NX)]
        pooled, masked = sem("pooled"), sem("masked")
        planes_out = sem("planes_out")
        tokens_out = sem("tokens_out")
        dve_pow, gp_pow = sem("dve_pow"), sem("gp_pow")
        a_ready, aT_ready, tT_ready = sem("a_ready"), sem("aT_ready"), sem("tT_ready")
        tm_ready = sem("tm_ready")
        max1 = sem("max1")
        x_ready = sem("x_ready")
        P1_ready = sem("P1_ready")
        uT_ready = sem("uT_ready")
        z_ready, zT_ready = sem("z_ready"), sem("zT_ready")
        gates_in, gates_exp = sem("gates_in"), sem("gates_exp")
        prob_ready, sel_rows, sel_ready = sem("prob_ready"), sem("sel_rows"), sem("sel_ready")
        u_ready = sem("u_ready")
        UT_ready = sem("UT_ready")
        hid_ready = sem("hid_ready")
        resid_ready = sem("resid_ready")
        hi_ready, lo_ready = sem("hi_ready"), sem("lo_ready")
        qk_out = sem("qk_out")
        stack_in = [sem(f"stack_in{s}") for s in range(NSTACK)]
        vals_ready = sem("vals_ready")
        peaks_ready = sem("peaks_ready")
        shift_ready = sem("shift_ready")
        shift_in = [sem(f"shift_in{s}") for s in range(2)]
        oT_ready = sem("oT_ready")
        rden_ready, onT_ready = sem("rden_ready"), sem("onT_ready")
        gated, fin_ready = sem("gated"), sem("fin_ready")
        out_done = [sem(f"out_done{s}") for s in range(2)]
        link = sem("link")
        waited = sem("waited")

        block = ctx.enter_context(nc.Block())

        class At:

            def __init__(self, section, g):
                self.section, self.g = section, g
                self.place, self.per = rings[section]
                before = {"pro": [], "loop": ["pro"], "last": ["pro"]}[section]
                self.turns = g if section == "loop" else (NG - 1 if section == "last" else 0)
                self.base = [sum(rings[s][1][k] for s in before) for k in range(MISC)]
                self.loop_per = rings["loop"][1]
                self.link_base = links["pro"] * len(before)
                self.links = 0

            def uses(self, key):
                slot, k = self.place[key]
                return slot, self.turns * self.loop_per[slot] + self.base[slot] + k

            def link_at(self, k):
                return self.turns * links["loop"] + self.link_base + self.links + k

        def run(eng, steps):
            def walk(section, g):
                at = At(section, g)
                for op in sections[section]:
                    if op[0] in steps:
                        steps[op[0]](at, g + op[1], *op[1:])
                    at.links += link_count(op)

            walk("pro", 0)
            if NG > 1:
                with eng.Fori(0, NG - 1) as g:
                    walk("loop", g)
            walk("last", NG - 1)

        def settled(eng):
            eng.sem_inc(waited, 1)

        turns = []
        for m in range(3):
            turns.append(([(wa_in[:, m, o, DC * c:DC * c + DC], DC * (2 * c + o), DC, DC)
                           for c in range(2) for o in range(2)], wa_T[:, m, :, :].rearrange("p c e -> p (c e)")))
        turns.append(([(wr_in[:, DC * c:DC * c + DC], E * c, E, DC) for c in range(2)],
                      RT[:, :, :].rearrange("p c e -> p (c e)")))
        turns.append(([(cwc[:, DC * c:DC * c + DC], C * c, C, DC) for c in range(2)],
                      cwcT[:, :, :].rearrange("p c e -> p (c e)")))
        for c in range(2):
            for f0 in range(0, 11, 4):
                fs = range(f0, min(f0 + 4, 11))
                end = min(128 * (fs[-1] + 1), F1)
                turns.append(([(w1_in[0:min(128, F1 - 128 * f), f, DC * c:DC * c + DC], 128 * (f - f0),
                                min(128, F1 - 128 * f), DC) for f in fs], w1T[:, c, 128 * f0:end]))
        for f0 in range(0, NF + 3, 2):
            fs = range(f0, min(f0 + 2, NF + 3))
            turns.append(([(w2_pad[:, o, 128 * f:128 * f + 128], D * (f - f0) + DC * o, DC, 128)
                           for f in fs for o in range(2)],
                          w2T[:, f0:fs[-1] + 1, :].rearrange("p f o -> p (f o)")))
        turns.append(([(Gc[:, DC * c:DC * c + DC], Z * c, Z, DC) for c in range(2)],
                      GcT[:, :, :].rearrange("p c e -> p (c e)")))
        NT = len(turns)

        @block.sync
        def _(sp):
            for s in [*peak_free, *score_free, *probs_used, *shift_in, *out_done, qk_out, gated, onT_ready, fin_ready]:
                sp.sem_inc(s, ONE)
            sp.dma_start(cst[:, :], consts).then_inc(cst_in, 16)
            for m, w in enumerate((Wq, Wk, Wv)):
                sp.dma_start(wa_in[:, m, :, :], w.rearrange("(o p) d -> p o d", p=DC)).then_inc(w_in, 16)
            sp.dma_start(cw_in[:, :], cw).then_inc(w_in, 16)
            sp.dma_start(G[0:C, :], cw).then_inc(w_in, 16)
            sp.dma_start(G[2 * C:Z, :], bv.rearrange("(a d) -> a d", a=1)).then_inc(w_in, 16)
            for m, b in enumerate((bq, bk)):
                for c in range(2):
                    sp.dma_start(QKp[:, m, c, 12:13], b[DC * c:DC * c + DC].rearrange("(p a) -> p a", a=1)) \
                        .then_inc(w_in, 16)
            sp.dma_start(wr_in[:, :], w_router).then_inc(w_in, 16)
            for m, b in enumerate((gamma, beta)):
                for c in range(2):
                    sp.dma_start(gb[:, m, c:c + 1], b[DC * c:DC * c + DC].rearrange("(p a) -> p a", a=1)) \
                        .then_inc(w_in, 16)
            sp.dma_start(w1_in[:, 0:10, :], w1[0:1280, :].rearrange("(f p) d -> p f d", p=128)).then_inc(w_in, 16)
            sp.dma_start(w1_in[0:F1 - 1280, 10, :], w1[1280:F1, :]).then_inc(w_in, 16)
            sp.dma_start(w2_in[:, :, :], w2.rearrange("(o p) f -> p o f", p=DC)).then_inc(w_in, 16)
            sp.dma_start(b1_in, b1.rearrange("(a f) -> a f", a=1)).then_inc(w_in, 16)
            sp.dma_start(b2_in[:, 0:2, :], b2.rearrange("(a o f) -> a o f", a=1, o=2)).then_inc(w_in, 16)
            sp.wait_ge(su_act, 2)
            sp.dma_start(G[C:2 * C, :], Vp).then_inc(su_dma, 16)
            sp.wait_ge(turn_free, NT - 1)
            sp.wait_ge(su_dve, 4)
            sp.dma_start(w2T[DH:DH + 1, NF, :], b2_in[:, 2, :]).then_inc(bias_in, 16)

            def project(at, G_, dg, i):
                n_ = G_ * GRP + i
                sp.wait_ge(hi_ready, 2 * n_ + 2)
                sp.wait_ge(lo_ready, 2 * n_ + 2)
                sp.dma_start(qk_dram[i % 2].rearrange("m s c p t -> p (m s c) t"),
                             qk16[:, :, :, :, :].rearrange("p m s c t -> p (m s c) t")).then_inc(qk_out, 16)
                sp.wait_ge(qk_out, 16 * n_ + 16 + ONE)
                s = i % NSTACK
                for blk, (qp, kp) in enumerate(((0, 0), (0, 1), (1, 0))):
                    for m, st, part in ((0, qs, qp), (1, ks, kp)):
                        sp.dma_start(st[DH * blk:DH * blk + DH, s, :, :],
                                     qk_dram[i % 2, m, part].rearrange("c (h d) t -> d (c h) t", d=DH)) \
                            .then_inc(stack_in[s], 16)

            def shift(at, G_, dg, i, part):
                n_ = G_ * GRP + i
                sp.wait_ge(shift_ready, 2 * n_ + part + 1)
                sp.dma_start(qs[KS:KS + 1, i % NSTACK, 6 * part:6 * part + 6, :],
                             shiftT[:, part, :]).then_inc(shift_in[part], 16)

            def fc2(at, G_, dg, i, k):
                if k == FC2 - 1:
                    n_ = G_ * GRP + i
                    sp.wait_ge(fin_ready, n_ + 1 + ONE)
                    sp.dma_start(out[bass.ds(n_, 1)].rearrange("a (h p) d -> p (a h) d", p=HT),
                                 fin[:, i % 2, :, :]).then_inc(out_done[i % 2], 16)

            run(sp, {"project": project, "shift": shift, "fc2": fc2})
            for s in range(2):
                sp.wait_ge(out_done[s], 16 * B // 2 + ONE)

        @block.tensor
        def _(pe):
            pe.wait_ge(cst_in, 16)
            pe.wait_ge(w_in, 16 * W_LOADS)
            for n_, (parts, dst) in enumerate(turns):
                if n_ == 4:
                    pe.wait_ge(su_dve, 1)
                if n_ == 11:
                    pe.wait_ge(su_dve, 2)
                if n_ == NT - 1:
                    pe.wait_ge(turn_free, 5)
                    for m in range(2):
                        for c in range(2):
                            for d in range(2):
                                mm = pe.matmul(banks[0][0:DC, 12 * (2 * m + c):12 * (2 * m + c) + 12],
                                               wa_T[:, m, d, DC * c:DC * c + DC], cwcT[:, d, :],
                                               start=(d == 0), stop=(d == 1))
                    mm.then_inc(su_pe, 1)
                    for d in range(2):
                        mm = pe.matmul(banks[1][0:C, 0:D], cwcT[:, d, :], wa_T[:, 2, d, :],
                                       start=(d == 0), stop=(d == 1))
                    mm.then_inc(su_pe, 1)
                    pe.wait_ge(su_dve, 5)
                if n_ >= MISC:
                    pe.wait_ge(turn_free, n_ - MISC + 1)
                for src, at_, r, w in parts:
                    mm = pe.transpose(misc_ps[n_ % MISC][0:w, at_:at_ + r], src, ident[0:r, 0:r])
                mm.then_inc(turn_full, 1)
            pe.wait_ge(turn_free, NT)
            pe.wait_ge(su_act, 1)
            for c in range(2):
                mm = pe.matmul(banks[2][0:13, 0:13], QKp[:, 0, c, :], QKp[:, 1, c, :],
                               start=(c == 0), stop=(c == 1))
            mm.then_inc(su_pe, 1)
            for c in range(2):
                mm = pe.matmul(banks[3][0:Z, 0:Z], GcT[:, c, :], GcT[:, c, :], start=(c == 0), stop=(c == 1))
            mm.then_inc(su_pe, 1)
            for c in range(2):
                mm = pe.matmul(banks[0][0:Z, 64:64 + E], GcT[:, c, :], RT[:, c, :],
                               start=(c == 0), stop=(c == 1))
            mm.then_inc(su_pe, 1)
            pe.wait_ge(su_dve, 6)
            pe.matmul(banks[1][:, 0:128], const("rep13", 13), A_rep[:, :, :].rearrange("p a b -> p (a b)"),
                      start=True, stop=True).then_inc(su_pe, 1)
            pe.matmul(banks[2][:, 128:276], const("rep25", Z), S_rep[:, :], start=True, stop=True) \
                .then_inc(su_pe, 1)
            pe.matmul(banks[3][:, 128:128 + D], const("rep25", Z), Gc, start=True, stop=True) \
                .then_inc(su_pe, 1)
            pe.matmul(banks[0][0:24, 128:152], const("rep12", C), S12[:, :], start=True, stop=True) \
                .then_inc(su_pe, 1)
            pe.wait_ge(su_dve, 7)
            for n3 in range(3):
                w = F1 // 3
                o = misc_ps[n3][0:U, 0:w]
                for c in range(2):
                    pe.matmul(o, L[:, c, :, :].rearrange("p e z -> p (e z)"), w1T[:, c, w * n3:w * n3 + w],
                              start=(c == 0), stop=False)
                mm = pe.matmul(o, const("last", 1), b1_in[:, w * n3:w * n3 + w], start=False, stop=True)
            mm.then_inc(su_pe, 1)
            pe.wait_ge(su_act, 3)
            pe.wait_ge(su_dve, 8)
            pe.wait_ge(bias_in, 16)
            pe.wait_ge(zeroed, 1)

            def ring(at, *key):
                slot, k = at.uses(key)
                pe.wait_ge(misc_free[slot], k)
                return misc_ps[slot], misc_full[slot]

            def planes(at, G_, dg, m):
                ps, full = ring(at, "planes", (dg, m))
                pe.wait_ge(masked, 4 * G_ + m + 1)
                for t in range(TILES):
                    mm = pe.matmul(ps[0:PAIR * C, 0:T],
                                   const("plane", PP)[:, PAIR * C * t:PAIR * C * t + PAIR * C],
                                   spread_p[:, t, :, :].rearrange("p a b -> p (a b)"),
                                   start=(t == 0), stop=(t == TILES - 1))
                mm.then_inc(full, 1)

            def tok(at, G_, dg, m):
                ps, full = ring(at, "tok", (dg, m))
                pe.wait_ge(planes_out, 4 * G_ + m + 1)
                for h in range(2):
                    mm = pe.matmul(ps[0:HT, 48 * h:48 * h + 48], planesT[:, HT * h:HT * h + HT], WI[:, :],
                                   start=True, stop=True)
                mm.then_inc(full, 1)

            def turn_x(at, key, ready, n_):
                ps, full = ring(at, *key)
                pe.wait_ge(ready, n_)
                for h in range(2):
                    mm = pe.transpose(ps[:, HT * h:HT * h + HT], x_tok[:, h, :, :], ident[0:HT, 0:HT])
                mm.then_inc(full, 1)

            def norm1_turn(at, G_, dg):
                turn_x(at, ("norm1_turn", (dg,)), a_ready, G_ + 1)

            def norm1_key(at, G_, dg):
                ps, full = ring(at, "norm1_key", (dg,))
                pe.wait_ge(aT_ready, 2 * G_ + 1)
                pe.matmul(ps[:, 0:T], Abd[:, 0, :], aT[:, :], start=True, stop=True).then_inc(full, 1)

            def first_max(at, G_, dg, i):
                ps, full = ring(at, "first_max", (dg, i))
                pe.wait_ge(tm_ready, 2 * GRP * G_ + i + 1)
                for h in range(2):
                    mm = pe.matmul(ps[0:HT, T * h:T * h + T], tm[:, i % 2, HT * h:HT * h + HT], aT[:, :],
                                   start=True, stop=True)
                mm.then_inc(full, 1)

            def shift1_turn(at, G_, dg):
                turn_x(at, ("shift1_turn", (dg,)), x_ready, G_ + 1)

            def shift1_key(at, G_, dg):
                ps, full = ring(at, "shift1_key", (dg,))
                pe.wait_ge(aT_ready, 2 * G_ + 2)
                pe.matmul(ps[:, 0:T], Abd[:, 1, :], xT[:, :], start=True, stop=True).then_inc(full, 1)

            def first_exp(at, G_, dg, i):
                ps, full = ring(at, "first_exp", (dg, i))
                pe.wait_ge(tm_ready, 2 * GRP * G_ + GRP + i + 1)
                for h in range(2):
                    mm = pe.matmul(ps[0:HT, T * h:T * h + T], aT[:, HT * h:HT * h + HT], tm[:, i % 2, :],
                                   start=True, stop=True)
                mm.then_inc(full, 1)

            def first_mix(at, G_, dg, i):
                j = 32 * (i % QUAD)
                slot, k = at.uses(("uT", (dg, i // QUAD)))
                if i % QUAD == 0:
                    pe.wait_ge(misc_free[slot], k)
                pe.wait_ge(P1_ready, GRP * G_ + i + 1)
                for h in range(2):
                    mm = pe.matmul(misc_ps[slot][j:j + 32, 0:T], a_tok[:, h, i, :], P1[:, i % 2, h, :],
                                   start=(h == 0), stop=(h == 1))
                if i % QUAD == QUAD - 1:
                    mm.then_inc(misc_full[slot], 1)

            def stream(at, G_, dg, q):
                ps, full = ring(at, "stream", (dg, q))
                pe.wait_ge(uT_ready, 2 * G_ + q + 1)
                for h in range(2):
                    mm = pe.transpose(ps[0:HT, 128 * h:128 * h + 128], uT[:, HT * h:HT * h + HT], ident)
                mm.then_inc(full, 1)

            def stream_turn(at, G_, dg, q):
                ps, full = ring(at, "stream_turn", (dg, q))
                pe.wait_ge(z_ready, 2 * G_ + q + 1)
                for h in range(2):
                    mm = pe.transpose(ps[:, HT * h:HT * h + HT], z_tok[:, h, QUAD * q:QUAD * q + QUAD, :],
                                      ident[0:HT, 0:HT])
                mm.then_inc(full, 1)

            def stream_norm(at, G_, dg, q):
                ps, full = ring(at, "stream_norm", (dg, q))
                pe.wait_ge(zT_ready, 2 * G_ + q + 1)
                for h in range(2):
                    mm = pe.matmul(ps[0:HT, 148 * h:148 * h + 148], zT[:, q, HT * h:HT * h + HT], WR[:, :],
                                   start=True, stop=True)
                mm.then_inc(full, 1)

            def gate_rows(at, G_, dg):
                ps, full = ring(at, "gate_rows", (dg,))
                pe.wait_ge(prob_ready, G_ + 1)
                for h in range(2):
                    mm = pe.transpose(ps[0:GRP * E, HT * h:HT * h + HT], prob[:, h, :], ident[0:HT, 0:HT])
                mm.then_inc(full, 1)

            def chosen(at, G_, dg):
                ps, full = ring(at, "chosen", (dg,))
                pe.wait_ge(sel_rows, G_ + 1)
                settled(pe)
                for h in range(2):
                    mm = pe.transpose(ps[0:HT, 32 * h:32 * h + 32], rows[:, HT * h:HT * h + HT],
                                      ident[0:32, 0:32])
                mm.then_inc(full, 1)

            def turn_u(at, G_, dg, i):
                ps, full = ring(at, "turn_u", (dg, i))
                pe.wait_ge(u_ready, G_ + 1)
                for h in range(2):
                    mm = pe.transpose(ps[0:U, HT * h:HT * h + HT],
                                      u_tok[:, GRP * h + i, :, :], ident[0:HT, 0:HT])
                mm.then_inc(full, 1)

            def residual(at, G_, dg, i):
                ps, full = ring(at, "residual", (dg, i))
                for h in range(2):
                    mm = pe.matmul(ps[0:HT, D * h:D * h + D], zT[:, i // QUAD, HT * h:HT * h + HT],
                                   G4[:, i % QUAD, :], start=True, stop=True)
                mm.then_inc(full, 1)

            def hidden(at, G_, dg, i):
                pe.wait_ge(UT_ready, GRP * G_ + i + 1)
                for b in range(NF // 2):
                    ps, full = ring(at, "hid", (dg, i, b))
                    for j in range(2):
                        f = 2 * b + j
                        mm = pe.matmul(ps[:, T * j:T * j + T], M[:, 128 * f:128 * f + 128], UT[:, i, :],
                                       start=True, stop=True)
                    mm.then_inc(full, 1)

            def project(at, G_, dg, i):
                pe.wait_ge(UT_ready, GRP * G_ + i + 1)
                for n_, m in enumerate("qk"):
                    ps, full = ring(at, m, (dg, i))
                    for c in range(2):
                        f = HID + D * n_ + DC * c
                        mm = pe.matmul(ps[0:DC, T * c:T * c + T], M[:, f:f + DC], UT[:, i, :],
                                       start=True, stop=True)
                    mm.then_inc(full, 1)

            def values(at, G_, dg, i):
                ps, full = ring(at, "values", (dg, i))
                for h in range(2):
                    mm = pe.matmul(ps[0:HT, D * h:D * h + D], UT[:, i, HT * h:HT * h + HT],
                                   M[:, HID + 2 * D:F1], start=True, stop=True)
                mm.then_inc(full, 1)

            def peak(at, G_, dg, i, h):
                s = h % 2
                if h == 0:
                    pe.wait_ge(stack_in[i % NSTACK], 96 * (2 * G_ + i // NSTACK + 1))
                pe.wait_ge(peak_free[s], 6 * (GRP * G_ + i) + h // 2 + ONE)
                for q in range(2):
                    mm = pe.matmul(peak_ps[s][0:HT, T * q:T * q + T],
                                   qs[0:KS, i % NSTACK, h, HT * q:HT * q + HT], ks[0:KS, i % NSTACK, h, :],
                                   start=True, stop=True)
                mm.then_inc(peak_full[s], 1)

            def shift(at, G_, dg, i, part):
                ps, full = ring(at, "shift", (dg, i, part))
                pe.wait_ge(peaks_ready, 2 * (GRP * G_ + i) + part + 1)
                for q in range(2):
                    mm = pe.transpose(ps[0:6, HT * q:HT * q + HT], peaks[:, part, q, :], ident[0:HT, 0:HT])
                mm.then_inc(full, 1)

            def score(at, G_, dg, i, h):
                s = h % 2
                if h % 6 == 0:
                    pe.wait_ge(shift_in[h // 6], 16 * (GRP * G_ + i + 1) + ONE)
                pe.wait_ge(score_free[s], 6 * (GRP * G_ + i) + h // 2 + ONE)
                for k in range(2):
                    mm = pe.matmul(score_ps[s][0:HT, T * k:T * k + T],
                                   ks[:, i % NSTACK, h, HT * k:HT * k + HT], qs[:, i % NSTACK, h, :],
                                   start=True, stop=True)
                mm.then_inc(score_full[s], 1)

            def mix(at, G_, dg, i, h):
                slot, k = at.uses(("O", (dg, i, h // 4)))
                if h % 4 == 0:
                    pe.wait_ge(misc_free[slot], k)
                if h == 0:
                    pe.wait_ge(vals_ready, GRP * G_ + i + 1)
                pe.wait_ge(score_free[h % 2], 6 * (GRP * G_ + i) + h // 2 + 1 + ONE)
                j = 32 * (h % 4)
                for q in range(2):
                    mm = pe.matmul(misc_ps[slot][j:j + 32, 0:T], vals[:, i % 2, q, h, :], Pb[:, h % NP, q, :],
                                   start=(q == 0), stop=(q == 1))
                mm.then_inc(probs_used[h % NP], 1)
                if h % 4 == 3:
                    pe.wait_ge(probs_used[h % NP], 3 * (GRP * G_ + i) + h // NP + 1 + ONE)
                    pe.sem_inc(misc_full[slot], 1)

            def norm(at, G_, dg, i, c):
                ps, full = ring(at, "norm", (dg, i, c))
                pe.wait_ge(oT_ready, 3 * (GRP * G_ + i) + c + 1)
                pe.matmul(ps[:, 0:T], const("den"), oT[:, c, :], start=True, stop=True).then_inc(full, 1)

            def fc2(at, G_, dg, i, k):
                slot, n_ = at.uses(("B", (dg, i)))
                if k == 0:
                    pe.wait_ge(misc_free[slot], n_)
                h, parts = k // 3, range(3 * (k % 3), 3 * (k % 3) + 3)
                if k == 2:
                    pe.wait_ge(onT_ready, 3 * (GRP * G_ + i) + 3 + ONE)
                for f in parts:
                    lhs = hid[:, i, f, HT * h:HT * h + HT] if f < NF else onT[:, f - NF, HT * h:HT * h + HT]
                    mm = pe.matmul(misc_ps[slot][0:HT, D * h:D * h + D], lhs, w2T[:, f, :],
                                   start=(f == 0), stop=(f == NF + 2))
                if k == FC2 - 1:
                    mm.then_inc(misc_full[slot], 1)

            run(pe, {"planes": planes, "tok": tok, "norm1_turn": norm1_turn, "norm1_key": norm1_key,
                     "first_max": first_max, "shift1_turn": shift1_turn, "shift1_key": shift1_key,
                     "first_exp": first_exp, "first_mix": first_mix, "stream": stream,
                     "stream_turn": stream_turn, "stream_norm": stream_norm, "gate_rows": gate_rows,
                     "chosen": chosen, "turn_u": turn_u, "residual": residual, "hidden": hidden,
                     "project": project, "values": values, "peak": peak, "shift": shift, "score": score,
                     "mix": mix, "norm": norm, "fc2": fc2})

        @block.scalar
        def _(act):
            for n_, (parts, dst) in enumerate(turns):
                if n_ == NT - 1:
                    act.wait_ge(su_pe, 1)
                    act.copy(QKp[:, :, :, 0:12], banks[0][0:DC, 0:48].rearrange("p (m c k) -> p m c k", m=2, c=2)) \
                        .then_inc(su_act, 1)
                    act.wait_ge(su_pe, 2)
                    act.copy(Vp, banks[1][0:C, 0:D]).then_inc(su_act, 1)
                act.wait_ge(turn_full, n_ + 1)
                rows_ = parts[0][3]
                cols = parts[-1][1] + parts[-1][2]
                act.copy(dst, misc_ps[n_ % MISC][0:rows_, 0:cols]).then_inc(turn_free, 1)
            act.wait_ge(su_pe, 10)
            for n3 in range(3):
                w = F1 // 3
                last = act.copy(M[:, w * n3:w * n3 + w], misc_ps[n3][0:U, 0:w])
            last.then_inc(su_act, 1)

            def ring(at, *key):
                slot, k = at.uses(key)
                act.wait_ge(misc_full[slot], k + 1)
                return misc_ps[slot], misc_free[slot]

            def load_tile(G_, t):
                first_plane = (G_ * (GRP // PAIR) + t // TILES) * PAIR * C + (t % TILES) * PLANES
                act.dma_start(xt[:, t % NX, :],
                              x.rearrange("b c (i k) w -> (b c i) (k w)", k=PATCH)
                              [bass.ds(first_plane * GRID, PP), :]).then_inc(x_in[t % NX], 16)

            def load(at, G_, dg):
                act.wait_ge(pooled, 12 * G_)
                for t in range(NX):
                    load_tile(G_, t)

            def fetch(at, G_, dg, m, t):
                act.wait_ge(pooled, 12 * G_ + TILES * m + t + 1)
                load_tile(G_, TILES * m + t + NX)

            def planes(at, G_, dg, m):
                ps, free = ring(at, "planes", (dg, m))
                evac(planesT[:, :], ps[0:PAIR * C, 0:T], free, planes_out, 4 * G_ + m + 1)

            def evac(dst, src, free, ready, n_):
                act.copy(dst, src).then_inc(ready, 1)
                act.wait_ge(ready, n_)
                act.sem_inc(free, 1)

            def norm1_turn(at, G_, dg):
                ps, free = ring(at, "norm1_turn", (dg,))
                evac(aT[:, :], ps[:, 0:T], free, aT_ready, 2 * G_ + 1)

            def norm1_key(at, G_, dg):
                ps, free = ring(at, "norm1_key", (dg,))
                evac(tT[:, :], ps[:, 0:T], free, tT_ready, 2 * G_ + 1)

            def shift1_turn(at, G_, dg):
                ps, free = ring(at, "shift1_turn", (dg,))
                evac(xT[:, :], ps[:, 0:T], free, aT_ready, 2 * G_ + 2)

            def shift1_key(at, G_, dg):
                ps, free = ring(at, "shift1_key", (dg,))
                act.wait_ge(tm_ready, 2 * GRP * G_ + GRP)
                evac(tT[:, :], ps[:, 0:T], free, tT_ready, 2 * G_ + 2)

            def first_exp(at, G_, dg, i):
                ps, free = ring(at, "first_exp", (dg, i))
                act.activation(P1[:, i % 2, :, :].rearrange("p a b -> p (a b)"), ps[0:HT, 0:2 * T], ACT.Exp,
                               scale=float(D) ** -0.5).then_inc(P1_ready, 1)
                act.wait_ge(P1_ready, GRP * G_ + i + 1)
                act.sem_inc(free, 1)

            def stream_sum(at, G_, dg, q):
                ps, free = ring(at, "uT", (dg, q))
                evac(uT[:, :], ps[:, 0:T], free, uT_ready, 2 * G_ + q + 1)

            def stream_turn(at, G_, dg, q):
                ps, free = ring(at, "stream_turn", (dg, q))
                evac(zT[:, q, :], ps[:, 0:T], free, zT_ready, 2 * G_ + q + 1)

            def gate_exp(at, G_, dg):
                act.wait_ge(gates_in, G_ + 1)
                act.activation(soft[:, 1, :], soft[:, 0, :], ACT.Exp).then_inc(gates_exp, 1)

            def residual(at, G_, dg, i):
                ps, free = ring(at, "residual", (dg, i))
                act.wait_ge(fin_ready, GRP * G_ + max(i - NRES + 1, 0) + ONE)
                for h in range(2):
                    last = act.activation(resid[:, i % NRES, h, :], ps[0:HT, D * h:D * h + D], ACT.Identity,
                                          bias=lg[:, h, i, 4:5], scale=var[:, 5, GRP * h + i:GRP * h + i + 1])
                last.then_inc(resid_ready, 1)
                act.wait_ge(resid_ready, GRP * G_ + i + 1)
                act.sem_inc(free, 1)

            def values(at, G_, dg, i):
                ps, free = ring(at, "values", (dg, i))
                evac(vals[:, i % 2, :, :, 0:DH], ps[0:HT, 0:2 * D].rearrange("p (a h d) -> p a h d", a=2, d=DH),
                     free, vals_ready, GRP * G_ + i + 1)

            def turn_u(at, G_, dg, i):
                ps, free = ring(at, "turn_u", (dg, i))
                evac(UT[:, i, :], ps[0:U, 0:T], free, UT_ready, GRP * G_ + i + 1)

            def hidden(at, G_, dg, i):
                for b in range(NF // 2):
                    ps, free = ring(at, "hid", (dg, i, b))
                    act.activation(hid[:, i, 2 * b:2 * b + 2, :].rearrange("p a b -> p (a b)"),
                                   ps[:, 0:2 * T], ACT.Gelu).then_inc(free, 1)

            def project(at, G_, dg, i):
                n_ = GRP * G_ + i
                act.wait_ge(qk_out, 16 * n_ + ONE)
                for m in range(2):
                    slot, k = at.uses(("qk"[m], (dg, i)))
                    act.wait_ge(misc_full[slot], k + 1)
                    act.copy(qk16[:, m, 0, :, :].rearrange("p c t -> p (c t)"), misc_ps[slot][0:DC, 0:2 * T]) \
                        .then_inc(hi_ready, 1)

            def shift(at, G_, dg, i, part):
                n_ = GRP * G_ + i
                ps, free = ring(at, "shift", (dg, i, part))
                act.wait_ge(shift_in[part], 16 * n_ + ONE)
                evac(shiftT[:, part, :], ps[0:6, 0:T], free, shift_ready, 2 * n_ + part + 1)

            def score(at, G_, dg, i, h):
                s = h % 2
                n_ = GRP * G_ + i
                act.wait_ge(score_full[s], 6 * n_ + h // 2 + 1)
                act.wait_ge(probs_used[h % NP], 3 * n_ + h // NP + ONE)
                act.activation(Pb[:, h % NP, :, :].rearrange("p a b -> p (a b)"), score_ps[s][0:HT, 0:2 * T],
                               ACT.Exp, scale=float(DH) ** -0.5).then_inc(score_free[s], 1)

            def mix(at, G_, dg, i, h):
                if h % 4 == 3:
                    c = h // 4
                    n_ = GRP * G_ + i
                    ps, free = ring(at, "O", (dg, i, c))
                    act.wait_ge(onT_ready, 3 * n_ + c + ONE)
                    evac(oT[:, c, :], ps[:, 0:T], free, oT_ready, 3 * n_ + c + 1)

            run(act, {"load": load, "fetch": fetch, "planes": planes, "norm1_turn": norm1_turn,
                      "norm1_key": norm1_key, "shift1_turn": shift1_turn, "shift1_key": shift1_key,
                      "first_exp": first_exp, "stream_sum": stream_sum, "stream_turn": stream_turn,
                      "gate_logits": gate_exp, "turn_u": turn_u, "residual": residual, "values": values,
                      "hidden": hidden, "project": project, "shift": shift, "score": score, "mix": mix})

        @block.vector
        def _(dve):
            dve.memset(qs[:, :, :, :], 0.0)
            dve.memset(vals[:, :, :, :, :], 1.0)
            dve.memset(z_tok[:, :, :, :], 0.0)
            dve.memset(a_tok[:, :, :, :], 0.0).then_inc(zeroed_dve, 1)
            dve.wait_ge(zeroed_dve, 1)
            dve.memset(a_tok[:, :, :, 12:14], 1.0)
            dve.memset(zs[:, :, :], 1.0)
            dve.memset(A_rep[:, :, :], 0.0)
            dve.memset(S_rep[:, :], 0.0)
            dve.memset(w2_pad, 0.0).then_inc(zeroed_dve, 1)
            dve.wait_ge(zeroed_dve, 2)
            dve.wait_ge(w_in, 16 * W_LOADS)
            dve.wait_ge(cst_in, 16)
            k = 2

            def done(ins):
                nonlocal k
                k += 1
                ins.then_inc(zeroed_dve, 1)
                dve.wait_ge(zeroed_dve, k)

            done(dve.tensor_reduce(mean[0:C, 0:1], cw_in[:, :], AX.X, ALU.add))
            done(dve.tensor_scalar(mean[0:C, 1:2], mean[0:C, 0:1], 1.0 / D, None, ALU.mult))
            dve.tensor_scalar(cwc[:, :], cw_in[:, :], mean[0:C, 1:2], None, ALU.subtract).then_inc(su_dve, 1)
            done(dve.tensor_tensor(w2_pad[:, :, 0:HID], w2_in[:, 0:2, 0:HID], w2_in[:, 2:4, 0:HID], ALU.add))
            for o in range(2):
                last = dve.tensor_tensor(
                    w2_pad[:, o, HID:].rearrange("p (h w) -> p h w", w=32)[:, :, 0:DH],
                    w2_in[:, o, HID:].rearrange("p (h w) -> p h w", w=DH),
                    w2_in[:, 2 + o, HID:].rearrange("p (h w) -> p h w", w=DH), ALU.add)
            last.then_inc(su_dve, 1)
            dve.tensor_tensor(b2_in[:, 2, :], b2_in[:, 0, :], b2_in[:, 1, :], ALU.add).then_inc(su_dve, 1)
            dve.memset(peaks[:, :, :, :], 0.0).then_inc(su_dve, 1)
            dve.wait_ge(su_dma, 16)
            done(dve.tensor_reduce(mean[:, 0:1], G, AX.X, ALU.add))
            done(dve.tensor_scalar(mean[:, 1:2], mean[:, 0:1], 1.0 / D, None, ALU.mult))
            dve.tensor_scalar(Gc, G, mean[:, 1:2], None, ALU.subtract).then_inc(su_dve, 1)
            dve.wait_ge(su_pe, 5)
            dve.tensor_copy(A_rep[:, :, 0:13], banks[2][0:13, 0:13].unsqueeze(1).broadcast_to([13, 8, 13]))
            dve.tensor_scalar(S_rep[:, 0:128].rearrange("p (a b) -> p a b", a=4)[:, :, 0:Z],
                              banks[3][0:Z, 0:Z].unsqueeze(1).broadcast_to([Z, 4, Z]), 1.0 / D, None, ALU.mult)
            dve.tensor_scalar(S12[:, :].rearrange("p (a b) -> p a b", a=2),
                              banks[3][0:C, 0:C].unsqueeze(1).broadcast_to([C, 2, C]), 1.0 / D, None, ALU.mult)
            dve.tensor_copy(S_rep[:, 128:148].rearrange("p (a b) -> p a b", a=4)[:, :, 0:E],
                            banks[0][0:Z, 64:64 + E].unsqueeze(1).broadcast_to([Z, 4, E]))
            dve.tensor_copy(S_rep[:, 128:148].rearrange("p (a b) -> p a b", a=4)[:, :, E:E + 1],
                            mean[:, 1:2].unsqueeze(1).broadcast_to([Z, 4, 1])).then_inc(su_dve, 1)
            dve.wait_ge(turn_free, NT)
            for c in range(2):
                dve.tensor_scalar(GgT[:, c, 0:Z], GcT[:, c, :], gb[:, 0, c:c + 1], None, ALU.mult)
                done(dve.tensor_copy(GgT[:, c, Z:ZS], gb[:, 1, c:c + 1]))
                last = dve.tensor_tensor(L[:, c, :, :], GgT[:, c, :].unsqueeze(1).broadcast_to([DC, E, ZS]),
                                         const("emask", DC)[:, E * c:E * c + E].unsqueeze(2)
                                         .broadcast_to([DC, E, ZS]), ALU.mult)
            last.then_inc(su_dve, 1)
            dve.wait_ge(su_pe, 9)
            done(dve.tensor_tensor(Abd[:, 0, :], banks[1][:, 0:128], const("mask8"), ALU.mult))
            dve.tensor_tensor(Abd[:, 1, :], Abd[:, 0, :], const("one13"), ALU.add)
            dve.tensor_tensor(WR[:, :], banks[2][:, 128:276], const("mask4"), ALU.mult)
            for j in range(QUAD):
                dve.tensor_scalar(G4[:, j, :], banks[3][:, 128:128 + D], const("col4")[:, j:j + 1], None,
                                  ALU.mult)
            dve.tensor_tensor(WI[:, 0:24], banks[0][0:24, 128:152], const("mask2", 24), ALU.mult)
            dve.tensor_copy(WI[:, 24:48], ident[0:24, 0:24]).then_inc(su_dve, 1)

            def ring(at, *key):
                slot, k_ = at.uses(key)
                dve.wait_ge(misc_full[slot], k_ + 1)
                return misc_ps[slot], misc_free[slot]

            state = [0]

            def chain(at, ins):
                state[0] += 1
                ins.then_inc(link, 1)
                dve.wait_ge(link, at.link_at(state[0]))

            def linked(op, count):
                assert state[0] == count, (op, state[0])
                state[0] = 0

            def pool(at, G_, dg, m, t, p):
                n_ = TILES * m + t
                if p == 0:
                    dve.wait_ge(x_in[n_ % NX], 16 * (TILES * (GRP // PAIR) // NX * G_ + n_ // NX + 1))
                    dve.wait_ge(masked, 4 * G_ + max(m - 1, 0))
                v = xt[:, n_ % NX, :].rearrange("p (k j w) -> p j k w", k=PATCH, w=PATCH)
                last = dve.tensor_reduce(psums[:, m % 2, t, 2 * p:2 * p + 2], v[:, 2 * p:2 * p + 2, :, :],
                                         AX.XY, ALU.add)
                if p == PIECES - 1:
                    last.then_inc(pooled, 1)

            def tok(at, G_, dg, m):
                ps, free = ring(at, "tok", (dg, m))
                v = ps[0:HT, 0:96].rearrange("p (h w b c) -> p h w b c", h=2, w=2, b=PAIR)
                dve.tensor_copy(wtok[:, :, PAIR * m:PAIR * m + PAIR, :], v[:, :, 0, :, :])
                dve.tensor_copy(z_tok[:, :, PAIR * m:PAIR * m + PAIR, 0:C], v[:, :, 1, :, :]).then_inc(free, 1)
                if m == GRP // PAIR - 1:
                    slot, k_ = at.uses(("tok", (dg, m)))
                    dve.wait_ge(misc_free[slot], k_ + 1)

            def norm1_scale(at, G_, dg):
                t12 = tmp[:, :, :, 0:C].rearrange("p h i c -> p (h i) c")
                chain(at, dve.tensor_tensor(t12, z_tok[:, :, :, 0:C].rearrange("p h i c -> p (h i) c"),
                                            wtok[:, :, :, :].rearrange("p h i c -> p (h i) c"), ALU.mult))
                chain(at, dve.tensor_reduce(var[:, 0, :], t12, AX.X, ALU.add))
                dve.tensor_scalar(var[:, 1, :], var[:, 0, :], 1e-5, None, ALU.add).then_inc(dve_pow, 1)
                linked("norm1_scale", 2)

            def norm1(at, G_, dg):
                dve.wait_ge(gp_pow, 3 * G_ + 1)
                chain(at, dve.tensor_tensor(
                    a_tok[:, :, :, 0:C].rearrange("p h i c -> p (h i) c"),
                    z_tok[:, :, :, 0:C].rearrange("p h i c -> p (h i) c"),
                    var[:, 2, :].unsqueeze(2).broadcast_to([HT, 2 * GRP, C]), ALU.mult))
                dve.tensor_copy(x_tok[:, :, :, :], a_tok[:, :, :, 0:16]).then_inc(a_ready, 1)
                linked("norm1", 1)

            def first_max(at, G_, dg, i):
                ps, free = ring(at, "first_max", (dg, i))
                dve.tensor_reduce(nm1[:, :, i], ps[0:HT, 0:2 * T].rearrange("p (h k) -> p h k", h=2),
                                  AX.X, ALU.max, negate=True).then_inc(free, 1)

            def shift1(at, G_, dg):
                slot, k_ = at.uses(("first_max", (dg, GRP - 1)))
                dve.wait_ge(misc_free[slot], k_ + 1)
                dve.wait_ge(a_ready, G_ + 1)
                chain(at, dve.tensor_copy(x_tok[:, :, :, 13], nm1[:, :, :]))
                chain(at, dve.tensor_copy(x_tok[:, :, :, 12], a_tok[:, :, :, 12]))
                dve.sem_inc(x_ready, 1)
                linked("shift1", 2)

            def stream(at, G_, dg, q):
                i = QUAD * q
                ps, free = ring(at, "stream", (dg, q))
                v = ps[0:HT, 0:256].rearrange("p (h i c) -> p h i c", h=2, i=QUAD)
                chain(at, dve.reciprocal(urec[:, :, :], v[:, :, :, 12]))
                for h in range(2):
                    last = dve.tensor_tensor(z_tok[:, h, i:i + QUAD, C:Z], v[:, h, :, 0:13],
                                             urec[:, h, :].unsqueeze(2).broadcast_to([HT, QUAD, 13]), ALU.mult)
                last.then_inc(z_ready, 1)
                dve.wait_ge(z_ready, 2 * G_ + q + 1)
                dve.sem_inc(free, 1)
                linked("stream", 1)

            def stream_norm(at, G_, dg, q):
                i = QUAD * q
                ps, free = ring(at, "stream_norm", (dg, q))
                v = ps[0:HT, 0:296].rearrange("p (h w) -> p h w", h=2)
                for h in range(2):
                    last = dve.tensor_tensor(tmp[:, h, i:i + QUAD, 0:Z],
                                             v[:, h, 0:128].rearrange("p (i c) -> p i c", i=QUAD)[:, :, 0:Z],
                                             z_tok[:, h, i:i + QUAD, 0:Z], ALU.mult)
                chain(at, last)
                chain(at, dve.tensor_reduce(var[:, 3, :].rearrange("p (h i) -> p h i", h=2)[:, :, i:i + QUAD],
                                            tmp[:, :, i:i + QUAD, 0:Z], AX.X, ALU.add))
                for h in range(2):
                    last = dve.tensor_copy(lg[:, h, i:i + QUAD, :],
                                           v[:, h, 128:148].rearrange("p (i e) -> p i e", i=QUAD))
                last.then_inc(free, 1)
                if q == 1:
                    slot, k_ = at.uses(("stream_norm", (dg, q)))
                    dve.wait_ge(misc_free[slot], k_ + 1)
                linked("stream_norm", 2)

            def wide(a):
                return a.unsqueeze(2).broadcast_to([HT, 2 * GRP, E])

            s0, s1, s2 = (soft[:, k_, :].rearrange("p (n e) -> p n e", e=E) for k_ in range(3))

            def gate_scale(at, G_, dg):
                dve.tensor_scalar(var[:, 1, :], var[:, 3, :], 1e-5, None, ALU.add).then_inc(dve_pow, 1)

            def gate_logits(at, G_, dg):
                lgv = lg[:, :, :, :].rearrange("p h i e -> p (h i) e")
                dve.wait_ge(gp_pow, 3 * G_ + 2)
                chain(at, dve.tensor_tensor(s2, lgv[:, :, 0:E], wide(var[:, 2, :]), ALU.mult))
                chain(at, dve.tensor_reduce(red[:, 0, :], s2, AX.X, ALU.max))
                chain(at, dve.tensor_tensor(s0, s2, wide(red[:, 0, :]), ALU.subtract))
                dve.sem_inc(gates_in, 1)
                dve.tensor_copy(var[:, 6, :], var[:, 2, :])
                chain(at, dve.tensor_tensor(var[:, 4, :], var[:, 2, :], var[:, 2, :], ALU.mult))
                chain(at, dve.tensor_tensor(var[:, 5, :], var[:, 4, :], var[:, 3, :], ALU.mult))
                dve.tensor_scalar(var[:, 1, :], var[:, 5, :], 1e-6, None, ALU.add).then_inc(dve_pow, 1)
                linked("gate_logits", 5)

            def gates(at, G_, dg):
                dve.wait_ge(gp_pow, 3 * G_ + 3)
                chain(at, dve.tensor_tensor(var[:, 7, :], var[:, 6, :], var[:, 2, :], ALU.mult))
                chain(at, dve.tensor_scalar(var[:, 5, :], var[:, 6, :], 1.0, None, ALU.add))
                dve.wait_ge(gates_exp, G_ + 1)
                chain(at, dve.tensor_reduce(red[:, 1, :], s1, AX.X, ALU.add))
                chain(at, dve.reciprocal(red[:, 2, :], red[:, 1, :]))
                pr = prob[:, :, :].rearrange("p h (i e) -> p (h i) e", e=E)
                chain(at, dve.tensor_tensor(pr, s1, wide(red[:, 2, :]), ALU.mult))
                dve.sem_inc(prob_ready, 1)
                linked("gates", 5)

            def gate_rows(at, G_, dg):
                ps, free = ring(at, "gate_rows", (dg,))
                chain(at, dve.tensor_copy(rows[:, :], ps[0:GRP * E, 0:T]))
                dve.sem_inc(free, 1)
                linked("gate_rows", 1)

            def choose(at, G_, dg, r):
                settled(dve)
                chain(at, dve.max(top8[:, :], rows[:, :]))
                if r == ROUNDS - 1:
                    chain(at, dve.memset(top8[:, CAP % 8:8], REPLACED))
                settled(dve)
                chain(at, dve.match_replace(rows[:, :], top8[:, :], rows[:, :], REPLACED))
                if r == ROUNDS - 1:
                    chain(at, dve.tensor_scalar(rows[:, :], rows[:, :], 0.0, None, ALU.is_lt))
                    dve.sem_inc(sel_rows, 1)
                linked("choose", link_count(("choose", 0, r)))

            def chosen(at, G_, dg):
                ps, free = ring(at, "chosen", (dg,))
                dve.tensor_copy(sel[:, :, :].rearrange("p h w -> p (h w)"), ps[0:HT, 0:64]).then_inc(sel_ready, 1)
                dve.wait_ge(sel_ready, G_ + 1)
                dve.sem_inc(free, 1)

            def spread(at, G_, dg):
                sv = sel[:, :, :].rearrange("p h (i e) -> p (h i) e", e=E)
                n_ = 2 * GRP
                dve.wait_ge(sel_ready, G_ + 1)
                chain(at, dve.tensor_tensor(zs[:, :, 0:Z], z_tok[:, :, :, 0:Z].rearrange("p h i c -> p (h i) c"),
                                            var[:, 7, :].unsqueeze(2).broadcast_to([HT, n_, Z]), ALU.mult))
                for e in range(E):
                    last = dve.tensor_tensor(u_tok[:, :, e, :], zs[:, :, :],
                                             sv[:, :, e:e + 1].broadcast_to([HT, n_, ZS]), ALU.mult)
                last.then_inc(u_ready, 1)
                linked("spread", 1)

            def gates8(at, G_, dg):
                sv = sel[:, :, :].rearrange("p h (i e) -> p (h i) e", e=E)
                pv = prob[:, :, :].rearrange("p h (i e) -> p (h i) e", e=E)
                n_ = 2 * GRP
                dve.wait_ge(gated, GRP * G_ + ONE)
                chain(at, dve.tensor_tensor(cg[:, :, :], sv, pv, ALU.mult))
                chain(at, dve.tensor_copy(gate8[:, :, 4:8], cg[:, :, 3:4].broadcast_to([HT, n_, 4])))
                chain(at, dve.tensor_tensor(gate8[:, :, 2:4], cg[:, :, 2:3].broadcast_to([HT, n_, 2]),
                                            gate8[:, :, 4:6], ALU.add))
                chain(at, dve.tensor_tensor(gate8[:, :, 1:2], cg[:, :, 1:2], gate8[:, :, 2:3], ALU.add))
                chain(at, dve.tensor_tensor(gate8[:, :, 0:1], cg[:, :, 0:1], gate8[:, :, 1:2], ALU.add))
                linked("gate8", 5)

            def project(at, G_, dg, i):
                for m in range(2):
                    slot, k_ = at.uses(("qk"[m], (dg, i)))
                    n_ = 2 * (GRP * G_ + i) + m + 1
                    dve.wait_ge(hi_ready, n_)
                    dve.tensor_tensor(qk16[:, m, 1, :, :].rearrange("p c t -> p (c t)"),
                                      misc_ps[slot][0:DC, 0:2 * T],
                                      qk16[:, m, 0, :, :].rearrange("p c t -> p (c t)"),
                                      ALU.subtract).then_inc(lo_ready, 1)
                    dve.wait_ge(lo_ready, n_)
                    dve.sem_inc(misc_free[slot], 1)

            def peak(at, G_, dg, i, h):
                s = h % 2
                n_ = 6 * (GRP * G_ + i) + h // 2 + 1
                dve.wait_ge(peak_full[s], n_)
                dve.tensor_reduce(peaks[:, h // 6, :, h % 6],
                                  peak_ps[s][0:HT, 0:2 * T].rearrange("p (q k) -> p q k", q=2),
                                  AX.X, ALU.max, negate=True).then_inc(peak_free[s], 1)
                if h % 6 == 5:
                    dve.wait_ge(peak_free[s], n_ + ONE)
                    dve.sem_inc(peaks_ready, 1)

            def norm(at, G_, dg, i, c):
                n_ = 3 * (GRP * G_ + i) + c
                ps, free = ring(at, "norm", (dg, i, c))
                dve.wait_ge(onT_ready, n_ + ONE)
                dve.reciprocal(rden[:, c, :], ps[:, 0:T]).then_inc(rden_ready, 1)
                dve.wait_ge(rden_ready, n_ + 1)
                dve.sem_inc(free, 1)

            def fc2(at, G_, dg, i, k_):
                if k_ == FC2 - 1:
                    n_ = GRP * G_ + i
                    ps, free = ring(at, "B", (dg, i))
                    dve.wait_ge(out_done[i % 2], 16 * (GRP // 2 * G_ + i // 2) + ONE)
                    for h in range(2):
                        last = dve.tensor_tensor(
                            fin[:, i % 2, h, :].rearrange("p (s w) -> p s w", s=8),
                            ps[0:HT, D * h:D * h + D].rearrange("p (s w) -> p s w", s=8),
                            gate8[:, GRP * h + i, :].unsqueeze(2).broadcast_to([HT, 8, D // 8]), ALU.mult)
                    last.then_inc(gated, 1)
                    dve.wait_ge(gated, n_ + 1 + ONE)
                    dve.sem_inc(free, 1)

            run(dve, {"pool": pool, "tok": tok, "norm1_scale": norm1_scale, "norm1": norm1,
                      "first_max": first_max, "shift1": shift1, "stream": stream, "stream_norm": stream_norm,
                      "gate_scale": gate_scale, "gate_logits": gate_logits, "gates": gates,
                      "gate_rows": gate_rows, "choose": choose, "chosen": chosen, "spread": spread,
                      "gate8": gates8, "project": project, "peak": peak, "norm": norm, "fc2": fc2})

        @block.gpsimd
        def _(pool_e):
            gp = pool_e
            gp.memset(ks[:, :, :, :], 0.0).then_inc(gp_in, 1)
            gp.wait_ge(gp_in, 1)
            gp.memset(ks[KS:KS + 1, :, :, :], 1.0).then_inc(zeroed, 1)
            gp.wait_ge(zeroed, 1)
            gp.wait_ge(cst_in, 16)

            def own_row(at, G_, dg, m, t):
                if t == 0:
                    gp.wait_ge(planes_out, 4 * G_ + m)
                gp.wait_ge(pooled, 12 * G_ + TILES * m + t + 1)
                last = gp.tensor_tensor(
                    spread_p[:, t, :, :],
                    psums[:, m % 2, t, :].unsqueeze(1).broadcast_to([PP, GRID, GRID]),
                    const("rowsel", PP).unsqueeze(2).broadcast_to([PP, GRID, GRID]), ALU.mult)
                if t == TILES - 1:
                    last.then_inc(masked, 1)

            def rsqrt(G_, n_):
                gp.wait_ge(dve_pow, 3 * G_ + n_)
                gp.tensor_tensor(var[:, 2, :], var[:, 1, :], const("half", HT), ALU.pow).then_inc(gp_pow, 1)

            def norm1_scale(at, G_, dg):
                rsqrt(G_, 1)

            def gate_scale(at, G_, dg):
                rsqrt(G_, 2)

            def gate_logits(at, G_, dg):
                rsqrt(G_, 3)

            def own_image(at, G_, dg, i, second):
                if i == 0:
                    gp.wait_ge(tT_ready, 2 * G_ + second + 1)
                if i >= 2:
                    slot, k_ = at.uses((("first_max", "first_exp")[second], (dg, i - 2)))
                    gp.wait_ge(misc_full[slot], k_ + 1)
                settled(gp)
                gp.tensor_scalar(tm[:, i % 2, :], tT[:, :], const("col8")[:, i:i + 1], 1.0, ALU.mult, ALU.mult) \
                    .then_inc(tm_ready, 1)

            def norm(at, G_, dg, i, c):
                n_ = 3 * (GRP * G_ + i) + c
                gp.wait_ge(rden_ready, n_ + 1)
                gp.wait_ge(gated, GRP * G_ + i + ONE)
                gp.tensor_tensor(onT[:, c, :], oT[:, c, :], rden[:, c, :], ALU.mult).then_inc(onT_ready, 1)

            def fc2(at, G_, dg, i, k_):
                if k_ == FC2 - 1:
                    n_ = GRP * G_ + i
                    gp.wait_ge(gated, n_ + 1 + ONE)
                    gp.wait_ge(resid_ready, n_ + 1)
                    gp.tensor_tensor(fin[:, i % 2, :, :], fin[:, i % 2, :, :], resid[:, i % NRES, :, :], ALU.add) \
                        .then_inc(fin_ready, 1)

            run(gp, {"own_row": own_row, "norm1_scale": norm1_scale, "gate_scale": gate_scale,
                     "gate_logits": gate_logits, "own_image": own_image, "norm": norm, "fc2": fc2})


_INS = ["x", "L0_tok_channel_weights", "L0_attn_Wq", "L0_attn_bq", "L0_attn_Wk", "L0_attn_bk", "L0_attn_Wv",
        "L0_attn_bv", "L0_ffn_w_router", "L0_ffn_gamma1", "L0_ffn_beta1", "L0_ffn_w1", "L0_ffn_b1",
        "L0_ffn_w2", "L0_ffn_b2"]


def kernel(**inputs):
    import concourse.bacc as _bacc
    from concourse.bass_utils import run_bass_kernel_spmd as _run

    nc = _bacc.Bacc("TRN2", target_bir_lowering=False, num_devices=1)
    arrays, args = {}, []
    for name in _INS:
        a = np.ascontiguousarray(inputs[name])
        arrays[f"in_{name}_dram"] = a
        args.append(nc.dram_tensor(f"in_{name}_dram", a.shape, mybir.dt.from_np(a.dtype), kind="ExternalInput").ap())
    arrays["in_consts_dram"] = constants()
    args.append(nc.dram_tensor("in_consts_dram", (128, NCONST), F32, kind="ExternalInput").ap())
    shape = (inputs["x"].shape[0], T, D)
    args.append(nc.dram_tensor("out_0_dram", shape, F32, kind="ExternalOutput").ap())
    bass_vit_tower(nc, *args)
    r = _run(nc, [arrays], core_ids=[0])
    return r.results[0]["out_0_dram"]
```
